# Optimizing a Trainium2 kernel written in Bass

```python
import numpy as np
import jax
import jax.numpy as jnp

def _softmax(x, axis=-1):
    return jax.nn.softmax(x, axis=axis)

def _gelu(x):
    return jax.nn.gelu(x, approximate=True)

def _silu(x):
    return jax.nn.silu(x)

def _sigmoid(x):
    return jax.nn.sigmoid(x)

def _layernorm(x, axis=-1, eps=1e-05):
    m = jnp.mean(x, axis=axis, keepdims=True)
    v = jnp.var(x, axis=axis, keepdims=True)
    return (x - m) / jnp.sqrt(v + eps)

def _scatter_add(tgt, idx, src, axis=0):
    return tgt.at[idx].add(src)

def _segment_sum(src, seg, n):
    return jax.ops.segment_sum(src, seg, n)
kernel_name = 'mk_lm_tower_d1_tok_ids1024_r4_56763c'

def setup_inputs(seed: int=0):
    np.random.seed(seed)
    _w = jnp.asarray

    def _rec_inputs():
        import jax
        import jax.numpy as jnp
        _rk = jax.random.key(seed)
        x = jax.random.randint(jax.random.fold_in(_rk, 1), (8, 1024), 0, 199957, jnp.int32)
        return x
    x = _rec_inputs()

    def _L0_tok_setup():
        import jax, jax.numpy as jnp
        import numpy as np
        CUTOFF_ENDS = [0, 12500, 25000, 45000, 50000]
        D_EMBED = 256
        D_PROJ = 256
        DIV_VAL = 4
        N_CLUSTERS = 4
        EMB_SCALE = D_PROJ ** 0.5
        key = jax.random.key(seed)
        ks = jax.random.split(key, 1 + 2 * N_CLUSTERS)
        inp = jax.random.randint(ks[0], (8, 512), 0, CUTOFF_ENDS[-1])
        d = {'inp': inp}
        for i in range(N_CLUSTERS):
            d_i = D_EMBED // DIV_VAL ** i
            size = CUTOFF_ENDS[i + 1] - CUTOFF_ENDS[i]
            d[f'emb{i}'] = jax.random.normal(ks[1 + i], (size, d_i), dtype=jnp.float32) * 0.02
            d[f'proj{i}'] = jax.random.normal(ks[1 + N_CLUSTERS + i], (D_PROJ, d_i), dtype=jnp.float32) * 0.02
        return d
    _L0_tok_all = _L0_tok_setup()
    _L0_tok_in = {k: v for k, v in _L0_tok_all.items() if k in ('emb0', 'emb1', 'emb2', 'emb3', 'proj0', 'proj1', 'proj2', 'proj3')}
    del _L0_tok_all

    def _L0_attn_setup():
        import jax, jax.numpy as jnp
        import numpy as np
        import math
        D = 256
        CHUNK = 64
        B = 4
        S = 1024

        def _layernorm(x, g, b, eps=1e-05):
            mu = jnp.mean(x, axis=-1, keepdims=True)
            var = jnp.mean((x - mu) ** 2, axis=-1, keepdims=True)
            return (x - mu) * jax.lax.rsqrt(var + eps) * g + b
        key = jax.random.key(seed)
        ks = jax.random.split(key, 8)
        lin = lambda k: jax.random.normal(k, (D, D), jnp.float32) * 0.02
        return {'x': jax.random.normal(ks[0], (B, S, D), jnp.float32), 'Wk': lin(ks[1]), 'bk': jnp.zeros((D,), jnp.float32), 'Wv': lin(ks[2]), 'bv': jnp.zeros((D,), jnp.float32), 'Wq': lin(ks[3]), 'bq': jnp.zeros((D,), jnp.float32), 'Wkp': lin(ks[4]), 'bkp': jnp.zeros((D,), jnp.float32), 'Wqp': lin(ks[5]), 'bqp': jnp.zeros((D,), jnp.float32), 'phase_scale': jnp.ones((D,), jnp.float32) * math.pi, 'ln_g': jnp.ones((D,), jnp.float32), 'ln_b': jnp.zeros((D,), jnp.float32), 'Wo': lin(ks[6]), 'bo': jnp.zeros((D,), jnp.float32)}
    _L0_attn_all = _L0_attn_setup()
    _L0_attn_in = {k: v for k, v in _L0_attn_all.items() if k in ('Wk', 'bk', 'Wv', 'bv', 'Wq', 'bq', 'Wkp', 'bkp', 'Wqp', 'bqp', 'phase_scale', 'ln_g', 'ln_b', 'Wo', 'bo')}
    del _L0_attn_all

    def _L0_ffn_setup():
        import jax, jax.numpy as jnp
        import numpy as np
        LN_EPS = 1e-05

        def layer_norm(x, g, b):
            mu = jnp.mean(x, axis=-1, keepdims=True)
            var = jnp.var(x, axis=-1, keepdims=True)
            return (x - mu) / jnp.sqrt(var + LN_EPS) * g + b

        def balanced_assignment(scores):
            T, E = scores.shape
            C = T // E
            taken = jnp.zeros((T,), dtype=bool)
            parts = []
            for e in range(E):
                s = jnp.where(taken, -jnp.inf, scores[:, e])
                _, idx = jax.lax.top_k(s, C)
                parts.append(idx)
                taken = taken.at[idx].set(True)
            return jnp.concatenate(parts)
        key = jax.random.key(seed)
        ks = jax.random.split(key, 4)
        B, S, D, F, E = (4, 512, 256, 1024, 8)
        return {'x': jax.random.normal(ks[0], (B, S, D), dtype=jnp.float32), 'centroids': jax.random.normal(ks[1], (E, D), dtype=jnp.float32) * 0.1, 'ln_g': jnp.ones((D,), dtype=jnp.float32), 'ln_b': jnp.zeros((D,), dtype=jnp.float32), 'w1': jax.random.normal(ks[2], (E, D, F), dtype=jnp.float32) * 0.02, 'b1': jnp.zeros((E, F), dtype=jnp.float32), 'w2': jax.random.normal(ks[3], (E, F, D), dtype=jnp.float32) * 0.02, 'b2': jnp.zeros((E, D), dtype=jnp.float32)}
    _L0_ffn_all = _L0_ffn_setup()
    _L0_ffn_in = {k: v for k, v in _L0_ffn_all.items() if k in ('centroids', 'ln_g', 'ln_b', 'w1', 'b1', 'w2', 'b2')}
    del _L0_ffn_all
    return {'x': x, 'L0_tok_emb0': _L0_tok_in['emb0'], 'L0_tok_emb1': _L0_tok_in['emb1'], 'L0_tok_emb2': _L0_tok_in['emb2'], 'L0_tok_emb3': _L0_tok_in['emb3'], 'L0_tok_proj0': _L0_tok_in['proj0'], 'L0_tok_proj1': _L0_tok_in['proj1'], 'L0_tok_proj2': _L0_tok_in['proj2'], 'L0_tok_proj3': _L0_tok_in['proj3'], 'L0_attn_Wk': _L0_attn_in['Wk'], 'L0_attn_bk': _L0_attn_in['bk'], 'L0_attn_Wv': _L0_attn_in['Wv'], 'L0_attn_bv': _L0_attn_in['bv'], 'L0_attn_Wq': _L0_attn_in['Wq'], 'L0_attn_bq': _L0_attn_in['bq'], 'L0_attn_Wkp': _L0_attn_in['Wkp'], 'L0_attn_bkp': _L0_attn_in['bkp'], 'L0_attn_Wqp': _L0_attn_in['Wqp'], 'L0_attn_bqp': _L0_attn_in['bqp'], 'L0_attn_phase_scale': _L0_attn_in['phase_scale'], 'L0_attn_ln_g': _L0_attn_in['ln_g'], 'L0_attn_ln_b': _L0_attn_in['ln_b'], 'L0_attn_Wo': _L0_attn_in['Wo'], 'L0_attn_bo': _L0_attn_in['bo'], 'L0_ffn_centroids': _L0_ffn_in['centroids'], 'L0_ffn_ln_g': _L0_ffn_in['ln_g'], 'L0_ffn_ln_b': _L0_ffn_in['ln_b'], 'L0_ffn_w1': _L0_ffn_in['w1'], 'L0_ffn_b1': _L0_ffn_in['b1'], 'L0_ffn_w2': _L0_ffn_in['w2'], 'L0_ffn_b2': _L0_ffn_in['b2']}

def reference(x, L0_tok_emb0, L0_tok_emb1, L0_tok_emb2, L0_tok_emb3, L0_tok_proj0, L0_tok_proj1, L0_tok_proj2, L0_tok_proj3, L0_attn_Wk, L0_attn_bk, L0_attn_Wv, L0_attn_bv, L0_attn_Wq, L0_attn_bq, L0_attn_Wkp, L0_attn_bkp, L0_attn_Wqp, L0_attn_bqp, L0_attn_phase_scale, L0_attn_ln_g, L0_attn_ln_b, L0_attn_Wo, L0_attn_bo, L0_ffn_centroids, L0_ffn_ln_g, L0_ffn_ln_b, L0_ffn_w1, L0_ffn_b1, L0_ffn_w2, L0_ffn_b2):
    import jax
    import jax.numpy as jnp

    def _L0_tok_ref(inp, emb0, emb1, emb2, emb3, proj0, proj1, proj2, proj3):
        import jax, jax.numpy as jnp
        import numpy as np
        CUTOFF_ENDS = [0, 12500, 25000, 45000, 50000]
        D_EMBED = 256
        D_PROJ = 256
        DIV_VAL = 4
        N_CLUSTERS = 4
        EMB_SCALE = D_PROJ ** 0.5
        tables = [emb0, emb1, emb2, emb3]
        projs = [proj0, proj1, proj2, proj3]
        flat = inp.reshape(-1)
        out = jnp.zeros((flat.shape[0], D_PROJ), dtype=jnp.float32)
        for i in range(N_CLUSTERS):
            l_idx, r_idx = (CUTOFF_ENDS[i], CUTOFF_ENDS[i + 1])
            mask = (flat >= l_idx) & (flat < r_idx)
            idx = jnp.clip(flat - l_idx, 0, r_idx - l_idx - 1)
            e = jnp.einsum('nd,pd->np', tables[i][idx], projs[i])
            out = jnp.where(mask[:, None], e, out)
        out = out.reshape(*inp.shape, D_PROJ) * jnp.float32(EMB_SCALE)
        return out

    def _L0_attn_ref(x, Wk, bk, Wv, bv, Wq, bq, Wkp, bkp, Wqp, bqp, phase_scale, ln_g, ln_b, Wo, bo):
        import jax, jax.numpy as jnp
        import numpy as np
        import math
        D = 256
        CHUNK = 64
        B = 4
        S = 1024

        def _layernorm(x, g, b, eps=1e-05):
            mu = jnp.mean(x, axis=-1, keepdims=True)
            var = jnp.mean((x - mu) ** 2, axis=-1, keepdims=True)
            return (x - mu) * jax.lax.rsqrt(var + eps) * g + b
        batch, seq_len, dim = x.shape
        key = jnp.einsum('bsd,ed->bse', x, Wk) + bk
        value = jnp.einsum('bsd,ed->bse', x, Wv) + bv
        query = jnp.einsum('bsd,ed->bse', x, Wq) + bq
        key_phase = jnp.tanh(jnp.einsum('bsd,ed->bse', key, Wkp) + bkp) * phase_scale
        query_phase = jnp.tanh(jnp.einsum('bsd,ed->bse', query, Wqp) + bqp) * phase_scale
        bound_real = value * jnp.cos(key_phase)
        bound_imag = value * jnp.sin(key_phase)
        pad_len = -seq_len % CHUNK
        if pad_len > 0:
            pad = ((0, 0), (0, pad_len), (0, 0))
            bound_real = jnp.pad(bound_real, pad)
            bound_imag = jnp.pad(bound_imag, pad)
            query_phase = jnp.pad(query_phase, pad)
        padded_len = seq_len + pad_len
        nc = padded_len // CHUNK
        br = bound_real.reshape(batch, nc, CHUNK, dim)
        bi = bound_imag.reshape(batch, nc, CHUNK, dim)
        qp = query_phase.reshape(batch, nc, CHUNK, dim)
        mem_real = jnp.cumsum(br, axis=2)
        mem_imag = jnp.cumsum(bi, axis=2)
        retrieved = mem_real * jnp.cos(qp) + mem_imag * jnp.sin(qp)
        retrieved = retrieved.reshape(batch, padded_len, dim)[:, :seq_len]
        retrieved = retrieved / math.sqrt(dim)
        out = jnp.einsum('bsd,ed->bse', _layernorm(retrieved, ln_g, ln_b), Wo) + bo
        return x + out

    def _L0_ffn_ref(x, centroids, ln_g, ln_b, w1, b1, w2, b2):
        import jax, jax.numpy as jnp
        import numpy as np
        LN_EPS = 1e-05

        def layer_norm(x, g, b):
            mu = jnp.mean(x, axis=-1, keepdims=True)
            var = jnp.var(x, axis=-1, keepdims=True)
            return (x - mu) / jnp.sqrt(var + LN_EPS) * g + b

        def balanced_assignment(scores):
            T, E = scores.shape
            C = T // E
            taken = jnp.zeros((T,), dtype=bool)
            parts = []
            for e in range(E):
                s = jnp.where(taken, -jnp.inf, scores[:, e])
                _, idx = jax.lax.top_k(s, C)
                parts.append(idx)
                taken = taken.at[idx].set(True)
            return jnp.concatenate(parts)
        D = x.shape[-1]
        feat = x.reshape(-1, D)
        T = feat.shape[0]
        E = centroids.shape[0]
        C = T // E
        norm = layer_norm(feat, ln_g, ln_b)
        scores = jax.lax.stop_gradient(norm @ centroids.T)
        sort_by_expert = balanced_assignment(scores)
        routed = feat[sort_by_expert].reshape(E, C, D)
        h = layer_norm(routed, ln_g, ln_b)
        h = jax.nn.gelu(jnp.einsum('ecd,edf->ecf', h, w1) + b1[:, None, :])
        h = jnp.einsum('ecf,efd->ecd', h, w2) + b2[:, None, :]
        out = routed + h
        inv = jnp.zeros((T,), dtype=jnp.int32).at[sort_by_expert].set(jnp.arange(T, dtype=jnp.int32))
        return out.reshape(T, D)[inv].reshape(x.shape)
    h = _L0_tok_ref(x, L0_tok_emb0, L0_tok_emb1, L0_tok_emb2, L0_tok_emb3, L0_tok_proj0, L0_tok_proj1, L0_tok_proj2, L0_tok_proj3)
    h = h + _L0_attn_ref(_layernorm(h, axis=-1), L0_attn_Wk, L0_attn_bk, L0_attn_Wv, L0_attn_bv, L0_attn_Wq, L0_attn_bq, L0_attn_Wkp, L0_attn_bkp, L0_attn_Wqp, L0_attn_bqp, L0_attn_phase_scale, L0_attn_ln_g, L0_attn_ln_b, L0_attn_Wo, L0_attn_bo)
    h = h + _L0_ffn_ref(_layernorm(h, axis=-1), L0_ffn_centroids, L0_ffn_ln_g, L0_ffn_ln_b, L0_ffn_w1, L0_ffn_b1, L0_ffn_w2, L0_ffn_b2)
    return h

_drawn_inputs = setup_inputs


def setup_inputs(seed=0):
    import zlib

    import numpy as np

    out = dict(_drawn_inputs(seed))
    spreads = {'L0_attn_bk': (0.0, 0.1),
     'L0_attn_bv': (0.0, 0.1),
     'L0_attn_bq': (0.0, 0.1),
     'L0_attn_bkp': (0.0, 0.1),
     'L0_attn_bqp': (0.0, 0.1),
     'L0_attn_phase_scale': (3.1415927410125732, 0.2),
     'L0_attn_ln_g': (1.0, 0.2),
     'L0_attn_ln_b': (0.0, 0.1),
     'L0_attn_bo': (0.0, 0.1),
     'L0_ffn_ln_g': (1.0, 0.2),
     'L0_ffn_ln_b': (0.0, 0.8),
     'L0_ffn_b1': (0.0, 0.337),
     'L0_ffn_b2': (0.0, 0.1)}
    factors = {}
    for name, (base, spread) in spreads.items():
        noise = np.random.default_rng([zlib.crc32(name.encode()), seed]).standard_normal(out[name].shape)
        drawn = base * np.exp(spread * noise) if base else spread * noise
        out[name] = jnp.asarray(drawn.astype(out[name].dtype))
    for name, factor in factors.items():
        out[name] = (out[name] * factor).astype(out[name].dtype)
    return out
```

```python
from collections import namedtuple
from contextlib import ExitStack
import math

import concourse.bass as bass
from concourse import mybir

F32 = mybir.dt.float32
BF16 = mybir.dt.bfloat16
I32 = mybir.dt.int32
U32 = mybir.dt.uint32
ALU = mybir.AluOpType
ACT = mybir.ActivationFunctionType
AX = mybir.AxisListType

P = 128
D = 256
KC = D // P
SUBS = 4
MT = SUBS * P
CHUNK = 64
EPS = 1e-5
ROW = D + 4
STEPS = 11
BIG = -3.0e38

Macro = namedtuple("Macro", "n half b")


def tower(nc, t):
    T = t["tok"].shape[0] * t["tok"].shape[1]
    NT = T // P
    NM = T // MT
    V, W = t["table"].shape
    E, _, F = t["w1"].shape
    C = T // E
    FC = F // P
    CT_ = C // P
    WCH = [(a, min(P, W - a)) for a in range(0, W, P)]
    assert C % MT == 0 and C // MT == 2 and W <= 3 * P

    h1_rows = nc.dram_tensor("h1_rows", (T, ROW), F32, kind="Internal").ap()

    ctx = ExitStack()
    with ctx:
        def sb(name, shape, dt=F32):
            return ctx.enter_context(nc.sbuf_tensor(name, shape, dt))

        def sem(name):
            return ctx.enter_context(nc.semaphore(name))

        banks = [ctx.enter_context(nc.psum_tensor(f"bank{i}", [P, 512], F32)) for i in range(8)]

        tok = sb("tok", [P, NT], I32)
        tokf = sb("tokf", [P, NT])
        tokm = sb("tokm", [P, NT])
        row_of = sb("row_of", [P, NT], I32)
        ident = sb("ident", [P, P])
        ones = sb("ones", [P, P])
        mean_w = sb("mean_w", [P, P])
        ones16 = sb("ones16", [P, P], BF16)
        later16 = sb("later16", [P, P], BF16)
        neg_half = sb("neg_half", [P, SUBS])
        eps = sb("eps", [P, SUBS])
        eps_r = sb("eps_r", [P, SUBS])
        plus1 = sb("plus1", [P, SUBS])
        minus1 = sb("minus1", [P, SUBS])
        half_pi = sb("half_pi", [P, 1])
        resets = sb("resets", [P, 2 * MT])
        proj = sb("proj", [P, 3, D])
        work = sb("work", [P, 4, 2, KC * MT])
        raw = work[:, :, :, :].rearrange("p a b m -> p (a b m)")
        wk, wq, wkpT, wqpT, woT, gwo = (raw[:, n * KC * D:(n + 1) * KC * D].rearrange("p (k n) -> p k n", k=KC)
                                        for n in range(6))
        wcomb = sb("wcomb", [P, 3, KC, D])
        wout = sb("wout", [P, KC, D])
        vecs = sb("vecs", [P, 10, KC])
        fbias = sb("fbias", [P, 2, KC])
        turns_of = sb("turns_of", [P, KC])
        lnb_bc = sb("lnb_bc", [P, KC, P])
        bo_bc = sb("bo_bc", [P, D])
        crow = sb("crow", [P, D])
        centT = sb("centT", [P, KC, E])
        BK, BV, BQ, BKP, BQP, PS, LG, LB, FG, FB = range(10)

        cur = sb("cur", [P, SUBS], I32)
        erow = sb("erow", [P, 2, SUBS, 344])
        eT = sb("eT", [P, 2, 3 * P])
        xhat = sb("xhat", [P, 2, SUBS, D])
        r1 = sb("r1", [P, 2, SUBS, D])
        xT = sb("xT", [P, KC, MT])
        tanh_, frac, sin_, cos_ = (work[:, n] for n in range(4))
        turns = sb("turns", [P, KC * MT], I32)
        fabs = sb("fabs", [P, KC * MT])
        bm = sb("bm", [P, 4, KC * MT])
        bound, mem = bm[:, 0:2], bm[:, 2:4]
        part = sb("part", [P, 2, KC * MT])
        ret = sb("ret", [P, KC, MT])
        hrow = sb("hrow", [P, 2, SUBS, ROW])
        nhat = sb("nhat", [P, SUBS, D])
        nT = sb("nT", [P, KC, MT])
        st_e = sb("st_e", [P, SUBS, 6])
        st_r = sb("st_r", [P, SUBS, 6])
        st_h = sb("st_h", [P, SUBS, 6])
        mv_e = sb("mv_e", [P, SUBS, 2])
        mv_r = sb("mv_r", [P, SUBS, 2])
        mv_h = sb("mv_h", [P, SUBS, 2])
        sc_e = sb("sc_e", [P, 4, SUBS])
        sc_r = sb("sc_r", [P, 2, SUBS])
        sc_h = sb("sc_h", [P, 8, SUBS])
        scores = sb("scores", [P, E, NT])

        w1s = sb("w1s", [P, 2, KC, F])
        w2s = sb("w2s", [P, 2, FC, D])
        b1s = sb("b1s", [P, 2, FC])
        b2s = sb("b2s", [P, 2, D])
        grow = hrow
        nb = nhat
        nbT = nT
        resb = r1
        hT = work[:, :, :, :].rearrange("p a b m -> p (a b m)").rearrange("p (k f m) -> p k f m", k=2, f=FC)
        orow = xhat
        iota_i = sb("iota_i", [P, P], I32)
        iota_b = sb("iota_b", [P, P], BF16)
        part_i = sb("part_i", [P, 1], I32)
        part_f = sb("part_f", [P, 1])
        tile_f = sb("tile_f", [P, NT])
        digits_i = sb("digits_i", [P, 8], I32)
        digits_f = sb("digits_f", [P, 8])
        steps = sb("steps", [P, STEPS, 7], U32)
        first = sb("first", [P, 3])
        flips = sb("flips", [P, 3], U32)
        taken = sb("taken", [P, NT])
        ones64 = sb("ones64", [P, NT])
        masked = sb("masked", [P, NT])
        cand = sb("cand", [P, 7], U32)
        above = sb("above", [P, 7, NT], BF16)
        cnt = sb("cnt", [P, 7])
        flag = sb("flag", [P, 7])
        digit = sb("digit", [P, 1])
        inc = sb("inc", [P, 3], U32)
        thr = sb("thr", [P, 1], U32)
        gteq = sb("gteq", [P, 2, NT], BF16)
        csum = sb("csum", [P, 2, NT])
        rank = sb("rank", [P, 2, NT])
        place = sb("place", [P, NT])
        sel = sb("sel", [P, 2, NT])
        slot = sb("slot", [P, NT], I32)
        slot_hi = sb("slot_hi", [P, NT], I32)
        slot_lo = sb("slot_lo", [P, NT], I32)
        onehot = bm[:, :, :].rearrange("p a m -> p (a m)").bitcast(BF16).rearrange("p (j m) -> p j m", m=P)
        lohot = sb("lohot", [P, NT, CT_], BF16)
        tokhot = sb("tokhot", [P, NT, 2 * CT_], BF16)
        listf = sb("listf", [P, 2 * CT_])
        lists = sb("lists", [P, 2, CT_], I32)

        names = """tok_loaded wts_loaded consts vec_loaded prep_dve prep_pe row_ready cur_ready
            eT_psum eT_ready h0_psum h0_stats h0_meanvar h0_steps h0_scales xhat_ready r1_summed r1_ready
            xT_psum xT_ready kqv_psum tanh_done turn_whole turn_frac turn_abs sin_ready cos_ready
            bound_ready mem_ready mr_cos mi_sin retrieved
            rT_psum r_stats r_meanvar r_steps r_scale wo_psum h1_ready h1_stats h1_meanvar row_steps row_scales
            nhat_ready nT_psum nT_ready scores_psum scores_saved pool_go dve_go
            cand_ready above_ready cnt_ready cnt_psum flag_ready inc_ready thr_ready thr_first
            masked_ready gteq_ready rank_psum place_steps taken_ready onehot_ready list_psum listf_ready list_ready
            nb_ready resb_ready nbT_psum nbT_ready mm1_psum gelu_done mm2_psum final_done sel_init""".split()
        S = namedtuple("Sems", names)(*[sem(n) for n in names])
        e_rows = [sem(f"e_rows{b}") for b in range(2)]
        h_stored = [sem(f"h_stored{b}") for b in range(2)]
        w_loaded = [sem(f"w_loaded{b}") for b in range(2)]
        g_rows = [sem(f"g_rows{b}") for b in range(2)]
        o_stored = [sem(f"o_stored{b}") for b in range(2)]

        block = ctx.enter_context(nc.Block())

        def pipeline(eng, step):
            def at(n, half, b):
                return Macro(n, half, b)

            def static(u):
                return Macro(u, u // 2, u % 2) if 0 <= u < NM else None

            for u in range(4):
                step(static(u), static(u - 1), static(u - 2), static(u + 1))
            with eng.Fori(0, (NM - 6) // 2) as j:
                for u in (4, 5):
                    step(at(2 * j + u, j + u // 2, u % 2), at(2 * j + u - 1, j + (u - 1) // 2, (u - 1) % 2),
                         at(2 * j + u - 2, j + (u - 2) // 2, u % 2), at(2 * j + u + 1, j + (u + 1) // 2, (u + 1) % 2))
            for u in range(NM - 2, NM + 2):
                step(static(u), static(u - 1), static(u - 2), static(u + 1))

        def experts(eng, step):
            step(0, 0, 0, True)
            with eng.Fori(0, (E - 2) // 2) as j:
                step(2 * j + 1, j, 1, True)
                step(2 * j + 2, j + 1, 0, True)
            step(E - 1, (E - 2) // 2, 1, False)

        def wait_after(eng, s, v):
            if not isinstance(v, int) or v > 0:
                eng.wait_ge(s, v)

        @block.sync
        def _(sp):
            sp.dma_start(tok[:, :], t["tok"]).then_inc(S.tok_loaded, 16)
            for dst, name in ((wk, "wk"), (wq, "wq"), (wkpT, "wkpT"), (wqpT, "wqpT"), (woT, "woT")):
                sp.dma_start(dst[:, :, :], t[name].rearrange("(k p) n -> p k n", p=P)).then_inc(S.wts_loaded, 16)
            sp.dma_start(wcomb[:, 2, :, :], t["wvT"].rearrange("(k p) n -> p k n", p=P)).then_inc(S.wts_loaded, 16)
            for k, (a, n) in enumerate(WCH):
                sp.dma_start(proj[0:n, k, :], t["projT"][a:a + n, :]).then_inc(S.wts_loaded, 16)
            sp.dma_start(centT[:, :, :], t["centT"].rearrange("(k p) n -> p k n", p=P)).then_inc(S.wts_loaded, 16)
            sp.dma_start(bo_bc[:, :], t["bo"].partition_broadcast(P)).then_inc(S.wts_loaded, 16)

            def load_expert(e, b):
                sp.dma_start(w1s[:, b, :, :], t["w1"][e].rearrange("(k p) f -> p k f", p=P)).then_inc(w_loaded[b], 16)
                sp.dma_start(w2s[:, b, :, :], t["w2"][e].rearrange("(k p) f -> p k f", p=P)).then_inc(w_loaded[b], 16)
                sp.dma_start(b1s[:, b, :], t["b1"][e]).then_inc(w_loaded[b], 16)
                sp.dma_start(b2s[:, b, :], t["b2"][e].partition_broadcast(P)).then_inc(w_loaded[b], 16)

            load_expert(0, 0)
            load_expert(1, 1)

            def store(embed, memory, mix, gather):
                if mix:
                    dst = h1_rows[bass.ds(mix.n * MT, MT), :].rearrange("(s p) c -> p s c", p=P)
                    sp.wait_ge(S.row_scales, mix.n + 1)
                    sp.wait_ge(S.row_scales, 1)
                    sp.dma_start(dst, hrow[:, mix.b, :, :]).then_inc(h_stored[mix.b], 16)

            pipeline(sp, store)
            for e in range(2, E):
                sp.wait_ge(S.mm2_psum, 8 * (e - 1))
                sp.wait_ge(S.final_done, 8 * (e - 1))
                load_expert(e, e % 2)
            for b in range(2):
                sp.wait_ge(o_stored[b], 16 * SUBS * E)

        @block.gpsimd
        def _(pl):
            cn = [0]

            def const(ins):
                cn[0] += 1
                ins.then_inc(S.consts, 1)
                return cn[0]

            const(pl.memset(ident[:, :], 0.0))
            const(pl.memset(later16[:, :], -1.0))
            const(pl.memset(resets[:, :], 1.0))
            const(pl.memset(ones[:, :], 1.0))
            const(pl.memset(mean_w[:, :], 1.0 / D))
            const(pl.memset(ones16[:, :], 1.0))
            const(pl.memset(neg_half[:, :], -0.5))
            const(pl.memset(eps[:, :], EPS))
            const(pl.memset(eps_r[:, :], D * EPS))
            const(pl.memset(plus1[:, :], 1.0))
            const(pl.memset(minus1[:, :], -1.0))
            const(pl.memset(half_pi[:, :], math.pi / 2))
            const(pl.memset(ones64[:, :], 1.0))
            const(pl.memset(taken[:, :], 0.0))
            const(pl.iota(iota_i[:, :], pattern=[[1, P]], base=0, channel_multiplier=0))
            const(pl.iota(part_i[:, :], pattern=[[0, 1]], base=0, channel_multiplier=1))
            const(pl.iota(digits_i[:, :], pattern=[[1, 8]], base=1, channel_multiplier=0))
            const(pl.memset(first[:, 0:1], -1.9999998807907104))
            const(pl.memset(first[:, 1:2], 0.0))
            n = const(pl.memset(first[:, 2:3], 2.0))
            pl.wait_ge(S.consts, n)
            const(pl.affine_select(out=ident[:, :], in_=ident[:, :], compare_op=ALU.not_equal, fill=1.0,
                                   base=0, pattern=[[-1, P]], channel_multiplier=1))
            const(pl.affine_select(out=later16[:, :], in_=later16[:, :], compare_op=ALU.is_gt, fill=0.0,
                                   base=0, pattern=[[-1, P]], channel_multiplier=1))
            const(pl.memset(resets[:, 0:2 * MT:CHUNK], 0.0))
            NCONST[0] = cn[0]

            def gather_rows(m):
                if isinstance(m.n, int):
                    src = row_of[:, m.n * SUBS:m.n * SUBS + SUBS]
                else:
                    src = row_of[:, bass.ds(m.n * SUBS, SUBS)]
                wait_after(pl, S.eT_psum, SUBS * (m.n - 1))
                if not isinstance(m.n, int) or m.n >= 2:
                    pl.wait_ge(e_rows[m.b], 16 * SUBS * m.half)
                if not isinstance(m.n, int) or m.n >= 1:
                    pl.wait_ge(e_rows[1 - m.b], 16 * SUBS * (m.half + m.b))
                pl.tensor_copy(cur[:, :], src).then_inc(S.cur_ready, 1)
                pl.wait_ge(S.cur_ready, m.n + 1)
                pl.sem_inc(S.pool_go, 1)
                for s in range(SUBS):
                    pl.indirect_dma_start(erow[:, m.b, s, 0:W], None, t["table"],
                                          bass.IndirectOffsetOnAxis(ap=cur[:, s:s + 1], axis=0)
                                          ).then_inc(e_rows[m.b], 16)

            def pw(out, in_):
                k = in_.shape[1]
                return pl.tensor_tensor(out, in_, neg_half[:, 0:k], ALU.pow)

            def embed_scales(m, pair):
                a = slice(2 * pair, 2 * pair + 2)
                pl.wait_ge(S.h0_meanvar, SUBS * m.n + 2 * pair + 2)
                base = [0]

                def link(ins):
                    _link(pl, S.h0_steps, 6 * m.n + 3 * pair, base, ins)
                link(pl.tensor_tensor(sc_e[:, 0, a], mv_e[:, a, 1], eps[:, 0:2], ALU.add))
                link(pw(sc_e[:, 1, a], sc_e[:, 0, a]))
                link(pl.tensor_tensor(sc_e[:, 2, a], mv_e[:, a, 0], minus1[:, 0:2], ALU.mult))
                pl.tensor_tensor(sc_e[:, 3, a], sc_e[:, 2, a], sc_e[:, 1, a], ALU.mult).then_inc(S.h0_scales, 1)

            def add_crow(m, pair):
                pl.wait_ge(S.r1_summed, 2 * m.n + pair + 1)
                for s in (2 * pair, 2 * pair + 1):
                    pl.tensor_tensor(r1[:, m.b, s, :], r1[:, m.b, s, :], crow[:, :], ALU.add
                                     ).then_inc(S.r1_ready, 1)

            def retrieved_scale(m):
                pl.wait_ge(S.r_meanvar, SUBS * (m.n + 1))
                base = [0]
                _link(pl, S.r_steps, m.n, base,
                      pl.tensor_tensor(sc_r[:, 0, :], mv_r[:, :, 1], eps_r[:, :], ALU.add))
                pw(sc_r[:, 1, :], sc_r[:, 0, :]).then_inc(S.r_scale, 1)

            def row_scalars(m):
                pl.wait_ge(S.h1_meanvar, SUBS * (m.n + 1))
                base = [0]
                mean, var = mv_h[:, :, 0], mv_h[:, :, 1]
                ve, rs, sq, v2, v3, rs2, nm = (sc_h[:, n, :] for n in range(7))

                def link(ins):
                    _link(pl, S.row_steps, 9 * m.n, base, ins)
                out = [hrow[:, m.b, :, D + n] for n in range(4)]
                link(pl.tensor_tensor(ve, var, eps[:, :], ALU.add))
                link(pw(rs, ve))
                link(pl.tensor_tensor(sq, rs, rs, ALU.mult))
                link(pl.tensor_tensor(v2, sq, var, ALU.mult))
                link(pl.tensor_tensor(v3, v2, eps[:, :], ALU.add))
                link(pw(rs2, v3))
                link(pl.tensor_tensor(nm, mean, minus1[:, :], ALU.mult))
                if not isinstance(m.n, int) or m.n >= 2:
                    pl.wait_ge(h_stored[m.b], 16 * m.half)
                link(pl.tensor_tensor(out[0], rs, rs2, ALU.mult))
                link(pl.tensor_tensor(out[2], rs, plus1[:, :], ALU.add))
                pl.tensor_tensor(out[3], nm, rs, ALU.mult)
                pl.tensor_tensor(out[1], nm, out[0], ALU.mult).then_inc(S.row_scales, 1)

            def imag_part(m):
                pl.wait_ge(S.mem_ready, 2 * m.n + 2)
                pl.wait_ge(S.sin_ready, 2 * m.n + 2)
                pl.tensor_tensor(part[:, 1, :], mem[:, 1, :], sin_[:, 1, :], ALU.mult).then_inc(S.mi_sin, 1)

            def step(embed, memory, mix, gather):
                if gather:
                    gather_rows(gather)
                if mix:
                    retrieved_scale(mix)
                if embed:
                    embed_scales(embed, 0)
                    add_crow(embed, 0)
                if mix:
                    row_scalars(mix)
                if embed:
                    embed_scales(embed, 1)
                    add_crow(embed, 1)
                if memory:
                    imag_part(memory)

            pl.wait_ge(S.row_ready, 4)
            gather_rows(Macro(0, 0, 0))
            pipeline(pl, step)

            def gather(k, b, lst, m, first_of_all=False):
                for s in range(SUBS):
                    pl.indirect_dma_start(grow[:, b, s, :], None, h1_rows,
                                          bass.IndirectOffsetOnAxis(ap=lists[:, lst, m * SUBS + s:m * SUBS + s + 1], axis=0)
                                          ).then_inc(g_rows[b], 16)

            def scatter(k, b, lst):
                pl.wait_ge(S.final_done, SUBS * (k + 1))
                pl.sem_inc(S.pool_go, 1)
                for s in range(SUBS):
                    pl.indirect_dma_start(t["out"], bass.IndirectOffsetOnAxis(ap=lists[:, lst, b * SUBS + s:b * SUBS + s + 1], axis=0),
                                          orow[:, b, s, :], None).then_inc(o_stored[b], 16)

            for b in range(2):
                pl.wait_ge(h_stored[b], 16 * (NM // 2))
            pl.wait_ge(S.list_ready, 1)
            gather(0, 0, 0, 0)

            def expert(e, half, b, more):
                gather(2 * e + 1, 1, b, 1)
                scatter(2 * e, 0, b)
                if more:
                    pl.wait_ge(S.list_ready, e + 2)
                    pl.sem_inc(S.pool_go, 1)
                    gather(2 * e + 2, 0, 1 - b, 0)
                scatter(2 * e + 1, 1, b)

            experts(pl, expert)

        @block.scalar
        def _(ac):
            for n, name in enumerate(("bk", "bv", "bq", "bkp", "bqp", "ps", "lg", "lb", "fg", "fb")):
                ac.dma_start(vecs[:, n, :], t[name]).then_inc(S.vec_loaded, 16)
            ac.preload_act_table_set("silu_and_others")
            ac.wait_ge(S.consts, NCONST[0])

            def ev_eT(m, s):
                ac.wait_ge(S.eT_psum, SUBS * m.n + s + 1)
                wait_after(ac, S.h0_psum, SUBS * m.n + s - 1)
                nfull = 2 * P
                ac.activation(eT[:, s % 2, 0:nfull], banks[s % 2][:, 0:nfull], ACT.Copy)
                ac.activation(eT[0:WCH[2][1], s % 2, nfull:nfull + P], banks[s % 2][0:WCH[2][1], nfull:nfull + P],
                              ACT.Copy).then_inc(S.eT_ready, 1)

            def make_xhat(m, pair):
                ac.wait_ge(S.h0_scales, 2 * m.n + pair + 1)
                for s in (2 * pair, 2 * pair + 1):
                    ac.activation(xhat[:, m.b, s, :], banks[2][:, (s % 2) * D:(s % 2 + 1) * D], ACT.Identity,
                                  scale=sc_e[:, 1, s:s + 1], bias=sc_e[:, 3, s:s + 1]).then_inc(S.xhat_ready, 1)

            def tanhs(m, kq):
                for c in range(KC):
                    n = 2 * kq + c
                    ac.wait_ge(S.kqv_psum, 6 * m.n + n + 1)
                    if n == 0:
                        wait_after(ac, S.turn_frac, 4 * m.n)
                    ac.activation(tanh_[:, kq, c * MT:(c + 1) * MT], banks[(5, 3, 4, 5)[n]][:, :], ACT.Tanh,
                                  bias=fbias[:, kq, c:c + 1]).then_inc(S.tanh_done, 1)

            def sincos(m, kq):
                if kq == 0:
                    wait_after(ac, S.bound_ready, 4 * m.n)
                else:
                    wait_after(ac, S.retrieved, m.n)
                ac.wait_ge(S.turn_frac, 4 * m.n + 2 * kq + 2)
                ac.activation(sin_[:, kq, :], frac[:, kq, :], ACT.Sin, scale=2 * math.pi).then_inc(S.sin_ready, 1)
                ac.wait_ge(S.turn_abs, 2 * m.n + kq + 1)
                ac.activation(cos_[:, kq, :], fabs[:, :], ACT.Sin, scale=-2 * math.pi,
                              bias=half_pi[:, 0:1]).then_inc(S.cos_ready, 1)

            def make_nhat(m):
                ac.wait_ge(S.row_scales, m.n + 1)
                wait_after(ac, S.nT_psum, 2 * m.n)
                for s in range(SUBS):
                    ac.activation(nhat[:, s, :], hrow[:, m.b, s, 0:D], ACT.Identity,
                                  scale=hrow[:, m.b, s, D:D + 1], bias=hrow[:, m.b, s, D + 1:D + 2]
                                  ).then_inc(S.nhat_ready, 1)

            def step(embed, memory, mix, gather):
                if embed:
                    ev_eT(embed, 0)
                    ev_eT(embed, 1)
                    make_xhat(embed, 0)
                if memory:
                    tanhs(memory, 0)
                if embed:
                    ev_eT(embed, 2)
                    ev_eT(embed, 3)
                if memory:
                    sincos(memory, 0)
                    tanhs(memory, 1)
                if mix:
                    make_nhat(mix)
                if memory:
                    sincos(memory, 1)
                if embed:
                    make_xhat(embed, 1)

            pipeline(ac, step)

            def expert(e, half, b, more):
                for m in range(2):
                    for f in range(FC):
                        n = FC * (2 * e + m) + f
                        ac.wait_ge(S.mm1_psum, n + 1)
                        ac.activation(hT[:, m, f, :], banks[f % 2 if FC % 3 else f % 3][:, :], ACT.Gelu_apprx_tanh,
                                      bias=b1s[:, b, f:f + 1]).then_inc(S.gelu_done, 1)

            experts(ac, expert)

        @block.vector
        def _(ve):
            pc = [0]

            def prep(ins):
                pc[0] += 1
                ins.then_inc(S.prep_dve, 1)
                ve.wait_ge(S.prep_dve, pc[0])

            ve.wait_ge(S.tok_loaded, 16)
            rows = V - 1

            def rl(ins, n):
                ins.then_inc(S.row_ready, 1)
                ve.wait_ge(S.row_ready, n)
            rl(ve.tensor_scalar(tokf[:, :], tok[:, :], float(-rows), None, ALU.add), 1)
            rl(ve.tensor_scalar(tokm[:, :], tokf[:, :], float(-rows), None, ALU.is_ge), 2)
            rl(ve.scalar_tensor_tensor(tokm[:, :], tokf[:, :], 0.0, tokm[:, :], ALU.is_lt, ALU.mult), 3)
            ve.tensor_tensor(tokf[:, :], tokf[:, :], tokm[:, :], ALU.mult).then_inc(S.sel_init, 1)
            ve.wait_ge(S.sel_init, 1)
            rl(ve.tensor_scalar(row_of[:, :], tokf[:, :], float(rows), None, ALU.add), 4)

            ve.wait_ge(S.wts_loaded, 16 * (8 + len(WCH)))
            ve.wait_ge(S.vec_loaded, 160)
            ve.wait_ge(S.consts, NCONST[0])
            for k, (a, n) in enumerate(WCH):
                prep(ve.tensor_scalar(proj[0:n, k, :], proj[0:n, k, :], math.sqrt(D), None, ALU.mult))
            prep(ve.tensor_scalar(turns_of[:, :], vecs[:, PS, :], 1.0 / (2 * math.pi), None, ALU.mult))
            for k in range(KC):
                prep(ve.tensor_scalar(gwo[:, k, :], woT[:, k, :], vecs[:, LG, k:k + 1], None, ALU.mult))
                prep(ve.tensor_scalar(lnb_bc[:, k, :], ones[:, :], vecs[:, LB, k:k + 1], None, ALU.mult))
            PREP_IN[0] = pc[0]
            ve.wait_ge(S.prep_pe, 4)
            for n in range(2):
                for k in range(KC):
                    prep(ve.tensor_copy(wcomb[:, n, k, :], banks[n][:, k * D:(k + 1) * D]))
                for k in range(KC):
                    prep(ve.tensor_tensor(fbias[:, n, k:k + 1], banks[2][:, 2 * n + k:2 * n + k + 1],
                                          vecs[:, BKP + n, k:k + 1], ALU.add))
            for k in range(KC):
                prep(ve.tensor_tensor(wout[:, k, :], gwo[:, k, :], banks[3][:, 0:D], ALU.subtract))
            prep(ve.tensor_tensor(crow[:, :], bo_bc[:, :], banks[3][:, D:2 * D], ALU.add))
            prep(ve.tensor_copy(iota_b[:, :], iota_i[:, :]))
            prep(ve.tensor_copy(part_f[:, :], part_i[:, :]))
            prep(ve.tensor_copy(tile_f[:, :], iota_i[:, 0:NT]))
            prep(ve.tensor_copy(digits_f[:, :], digits_i[:, :]))
            for v in range(1, STEPS):
                prep(ve.tensor_scalar(steps[:, v, :], digits_f[:, 0:7], float(1 << (30 - 3 * v)), None, ALU.mult))
            for n, bits in enumerate((1 << 30, 0, 1 << 30)):
                if n != 1:
                    prep(ve.tensor_scalar(flips[:, n:n + 1], digits_f[:, 0:1], float(bits), None, ALU.mult))
            prep(ve.tensor_scalar(flips[:, 1:2].bitcast(I32), digits_f[:, 0:1], -float(1 << 30), None, ALU.mult))
            prep(ve.tensor_scalar(flips[:, 1:2].bitcast(I32), flips[:, 1:2].bitcast(I32), (1 << 31) - 1, None,
                                  ALU.bitwise_xor))
            PREP_ALL[0] = pc[0]

            def stats(m, subs, psum_sem, stat_sem, mv_sem, src, st, mv):
                for s in subs:
                    if s % 2 == 0:
                        ve.wait_ge(psum_sem, SUBS * m.n + s + 2)
                    ve.bn_stats(st[:, s, :], src(s)).then_inc(stat_sem, 1)
                ve.wait_ge(stat_sem, SUBS * m.n + subs[-1] + 1)
                ve.sem_inc(S.dve_go, 1)
                for s in subs:
                    ve.bn_aggr(mv[:, s, :], st[:, s, :]).then_inc(mv_sem, 1)

            def pair_of(bank, s):
                return banks[bank][:, (s % 2) * D:(s % 2 + 1) * D]

            def embed_stats(m, pair):
                stats(m, [2 * pair, 2 * pair + 1], S.h0_psum, S.h0_stats, S.h0_meanvar,
                      lambda s: pair_of(2, s), st_e, mv_e)

            def embed_residual(m, pair):
                ve.wait_ge(S.xhat_ready, SUBS * m.n + 2 * pair + 2)
                ve.tensor_tensor(r1[:, m.b, 2 * pair:2 * pair + 2, :],
                                 banks[2][:, :].rearrange("p (s d) -> p s d", s=2),
                                 xhat[:, m.b, 2 * pair:2 * pair + 2, :], ALU.add).then_inc(S.r1_summed, 1)

            def evac_xT(m):
                for k in range(KC):
                    ve.wait_ge(S.xT_psum, 2 * m.n + k + 1)
                    ve.tensor_copy(xT[:, k, :], banks[3 + k][:, :]).then_inc(S.xT_ready, 1)

            def phase_turns(m, kq):
                for c in range(KC):
                    a = slice(c * MT, (c + 1) * MT)
                    n = 2 * kq + c
                    ve.wait_ge(S.tanh_done, 4 * m.n + n + 1)
                    wait_after(ve, S.turn_frac, 4 * m.n + n - 1)
                    ve.tensor_scalar(turns[:, a], tanh_[:, kq, a], turns_of[:, c:c + 1], None, ALU.mult
                                     ).then_inc(S.turn_whole, 1)
                if kq == 0:
                    wait_after(ve, S.sin_ready, 2 * m.n - 1)
                else:
                    wait_after(ve, S.sin_ready, 2 * m.n)
                for c in range(KC):
                    a = slice(c * MT, (c + 1) * MT)
                    n = 2 * kq + c
                    ve.wait_ge(S.turn_whole, 4 * m.n + n + 1)
                    ve.scalar_tensor_tensor(frac[:, kq, a], tanh_[:, kq, a], turns_of[:, c:c + 1], turns[:, a],
                                            ALU.mult, ALU.subtract).then_inc(S.turn_frac, 1)
                ve.wait_ge(S.turn_frac, 4 * m.n + 2 * kq + 2)
                wait_after(ve, S.cos_ready, 2 * m.n + kq)
                ve.tensor_scalar(fabs[:, :].bitcast(I32), frac[:, kq, :].bitcast(I32), (1 << 31) - 1, None,
                                 ALU.bitwise_and).then_inc(S.turn_abs, 1)

            def bind_and_sum(m):
                ve.wait_ge(S.cos_ready, 2 * m.n + 1)
                for c in range(KC):
                    a = slice(c * MT, (c + 1) * MT)
                    ve.wait_ge(S.kqv_psum, 6 * m.n + 5 + c)
                    for n, trig in enumerate((cos_, sin_)):
                        ve.scalar_tensor_tensor(bound[:, n, a], banks[3 + c][:, :], vecs[:, BV, c:c + 1], trig[:, 0, a],
                                                ALU.add, ALU.mult).then_inc(S.bound_ready, 1)
                ve.wait_ge(S.bound_ready, 4 * m.n + 4)
                wait_after(ve, S.mi_sin, m.n)
                for n in (1, 0):
                    ve.tensor_tensor_scan(mem[:, n, :], resets[:, :], bound[:, n, :], 0.0, ALU.mult, ALU.add
                                          ).then_inc(S.mem_ready, 1)

            def retrieve(m):
                ve.wait_ge(S.mem_ready, 2 * m.n + 2)
                ve.wait_ge(S.cos_ready, 2 * m.n + 2)
                ve.tensor_tensor(part[:, 0, :], mem[:, 0, :], cos_[:, 1, :], ALU.mult).then_inc(S.mr_cos, 1)
                ve.wait_ge(S.mr_cos, m.n + 1)
                ve.wait_ge(S.mi_sin, m.n + 1)
                wait_after(ve, S.wo_psum, SUBS * m.n)
                ve.tensor_tensor(ret[:, :, :].rearrange("p k m -> p (k m)"), part[:, 0, :], part[:, 1, :], ALU.add
                                 ).then_inc(S.retrieved, 1)

            def retrieved_stats(m):
                stats(m, list(range(SUBS)), S.rT_psum, S.r_stats, S.r_meanvar,
                      lambda s: pair_of(6 + s // 2, s), st_r, mv_r)

            def mix_residual(m, pair):
                ve.wait_ge(S.r_scale, m.n + 1)
                ve.wait_ge(S.r1_ready, SUBS * m.n + 2 * pair + 2)
                if not isinstance(m.n, int) or m.n >= 2:
                    ve.wait_ge(h_stored[m.b], 16 * m.half)
                ve.wait_ge(S.wo_psum, SUBS * m.n + 2 * pair + 2)
                for s in (2 * pair, 2 * pair + 1):
                    ve.scalar_tensor_tensor(hrow[:, m.b, s, 0:D], pair_of(6 + s // 2, s), sc_r[:, 1, s:s + 1],
                                            r1[:, m.b, s, :], ALU.mult, ALU.add).then_inc(S.h1_ready, 1)
                stats(m, [2 * pair, 2 * pair + 1], S.h1_ready, S.h1_stats, S.h1_meanvar,
                      lambda s: hrow[:, m.b, s, 0:D], st_h, mv_h)

            def evac_nT(m):
                for k in range(KC):
                    ve.wait_ge(S.nT_psum, 2 * m.n + k + 1)
                    if k == 0:
                        wait_after(ve, S.scores_psum, m.n)
                    ve.tensor_scalar(nT[:, k, :], banks[6 + k][:, :], vecs[:, FG, k:k + 1], vecs[:, FB, k:k + 1],
                                     ALU.mult, ALU.add).then_inc(S.nT_ready, 1)

            def save_scores(m):
                ve.wait_ge(S.scores_psum, m.n + 1)
                dst = scores[:, :, m.n * SUBS:m.n * SUBS + SUBS] if isinstance(m.n, int) else \
                    scores[:, :, bass.ds(m.n * SUBS, SUBS)]
                ve.tensor_copy(dst, banks[7][:, 0:SUBS * E].rearrange("p (s e) -> p e s", e=E)
                               ).then_inc(S.scores_saved, 1)

            def step(embed, memory, mix, gather):
                if mix:
                    retrieved_stats(mix)
                if memory:
                    evac_xT(memory)
                if embed:
                    embed_stats(embed, 0)
                if mix:
                    mix_residual(mix, 0)
                if embed:
                    embed_residual(embed, 0)
                if memory:
                    phase_turns(memory, 0)
                if mix:
                    mix_residual(mix, 1)
                if memory:
                    phase_turns(memory, 1)
                if embed:
                    embed_stats(embed, 1)
                if mix:
                    evac_nT(mix)
                if embed:
                    embed_residual(embed, 1)
                if mix:
                    save_scores(mix)
                if memory:
                    bind_and_sum(memory)
                    retrieve(memory)

            pipeline(ve, step)

            def begin_search(q):
                ve.wait_ge(S.taken_ready, q) if not isinstance(q, int) or q else ve.wait_ge(S.scores_saved, NM)
                src = scores[:, q, :] if isinstance(q, int) else scores[:, bass.ds(q, 1), :].rearrange("p a n -> p (a n)")
                ve.scalar_tensor_tensor(masked[:, :], taken[:, :], BIG, src, ALU.mult, ALU.add
                                        ).then_inc(S.masked_ready, 1)
                ve.wait_ge(S.masked_ready, q + 1)

            def count_above(q, v):
                n = 3 if v == 0 else 7
                if v:
                    ve.tensor_scalar(cand[:, :], steps[:, v, :], thr[:, 0:1], None, ALU.bitwise_xor
                                     ).then_inc(S.cand_ready, 1)
                    ve.wait_ge(S.cand_ready, (STEPS - 1) * q + v)
                c = first[:, :] if v == 0 else cand[:, :].bitcast(F32)
                ve.tensor_tensor(above[:, 0:n, :], masked[:, :].unsqueeze(1).broadcast_to([P, n, NT]),
                                 c.unsqueeze(2).broadcast_to([P, n, NT]), ALU.is_ge).then_inc(S.above_ready, 1)
                ve.wait_ge(S.above_ready, STEPS * q + v + 1)
                ve.tensor_reduce(cnt[:, 0:n], above[:, 0:n, :], AX.X, ALU.add).then_inc(S.cnt_ready, 1)

            def take_digit(q, v):
                ve.wait_ge(S.cnt_psum, STEPS * q + v + 1)
                if v == 0:
                    ve.tensor_scalar(inc[:, :].bitcast(I32), banks[7][:, 0:3], C - 0.5, -1.0, ALU.is_ge, ALU.mult
                                     ).then_inc(S.thr_first, 1)
                    ve.wait_ge(S.thr_first, 3 * q + 1)
                    ve.tensor_tensor(inc[:, :], inc[:, :], flips[:, :], ALU.bitwise_and).then_inc(S.thr_first, 1)
                    ve.wait_ge(S.thr_first, 3 * q + 2)
                    ve.scalar_tensor_tensor(thr[:, :].bitcast(I32), inc[:, 0:1].bitcast(I32), -1,
                                            inc[:, 1:2].bitcast(I32), ALU.bitwise_xor,
                                            ALU.bitwise_xor).then_inc(S.thr_first, 1)
                    ve.wait_ge(S.thr_first, 3 * q + 3)
                    ve.tensor_tensor(thr[:, :], thr[:, :], inc[:, 2:3], ALU.bitwise_xor).then_inc(S.thr_ready, 1)
                else:
                    ve.tensor_scalar(flag[:, :], banks[7][:, 0:7], C - 0.5, None, ALU.is_ge, ALU.add,
                                     accum_out=digit[:, 0:1]).then_inc(S.flag_ready, 1)
                    ve.wait_ge(S.flag_ready, (STEPS - 1) * q + v)
                    ve.tensor_scalar(inc[:, 0:1], digit[:, :], float(1 << (30 - 3 * v)), None, ALU.mult
                                     ).then_inc(S.inc_ready, 1)
                    ve.wait_ge(S.inc_ready, (STEPS - 1) * q + v)
                    ve.tensor_tensor(thr[:, :], thr[:, :], inc[:, 0:1], ALU.bitwise_xor).then_inc(S.thr_ready, 1)
                ve.wait_ge(S.thr_ready, STEPS * q + v + 1)

            def mark(q):
                T_ = thr[:, 0:1].bitcast(F32)
                ve.tensor_scalar(gteq[:, 0, :], masked[:, :], T_, None, ALU.is_gt).then_inc(S.gteq_ready, 1)
                ve.tensor_scalar(gteq[:, 1, :], masked[:, :], T_, None, ALU.is_equal).then_inc(S.gteq_ready, 1)

            def place_tokens(q):
                base = [0]

                def link(ins):
                    _link(ve, S.place_steps, 13 * q, base, ins)
                ve.wait_ge(S.rank_psum, q + 1)
                rk = banks[7][:, 128:128 + 4 * NT].rearrange("p (a g n) -> p a g n", a=2, g=2)
                for g in range(2):
                    link(ve.tensor_tensor_scan(csum[:, g, :], ones64[:, :], rk[:, 1, g, :], 0.0, ALU.mult, ALU.add))
                link(ve.tensor_tensor(rank[:, :, :], csum[:, :, :], rk[:, 0, :, :], ALU.add))
                link(ve.tensor_scalar(rank[:, 1, :], rank[:, 1, :], csum[:, 0, NT - 1:NT], None, ALU.add))
                link(ve.tensor_tensor(rank[:, :, :], rank[:, :, :], gteq[:, :, :], ALU.mult))
                link(ve.tensor_tensor(place[:, :], rank[:, 0, :], rank[:, 1, :], ALU.add))
                link(ve.tensor_scalar(sel[:, 0, :], place[:, :], 0.5, None, ALU.is_ge))
                link(ve.scalar_tensor_tensor(sel[:, 1, :], place[:, :], C + 0.5, sel[:, 0, :], ALU.is_le, ALU.mult))
                ve.tensor_tensor(taken[:, :], taken[:, :], sel[:, 1, :], ALU.add).then_inc(S.taken_ready, 1)
                link(ve.scalar_tensor_tensor(place[:, :], sel[:, 1, :], -4.0 * C, place[:, :], ALU.mult, ALU.add))
                link(ve.tensor_scalar(slot[:, :], place[:, :], 4.0 * C - 1.0, None, ALU.add))
                link(ve.tensor_scalar(slot_hi[:, :], slot[:, :], P - 1, None, ALU.bitwise_and))
                link(ve.tensor_scalar(slot_lo[:, :], slot[:, :], int(math.log2(P)), None, ALU.logical_shift_right))
                link(ve.tensor_tensor(lohot[:, :, :], iota_b[:, 0:CT_].unsqueeze(1).broadcast_to([P, NT, CT_]),
                                      slot_lo[:, :].unsqueeze(2).broadcast_to([P, NT, CT_]), ALU.is_equal))
                ve.tensor_scalar(tokhot[:, :, 0:CT_], lohot[:, :, :], part_f[:, 0:1], None, ALU.mult)
                ve.tensor_tensor(tokhot[:, :, CT_:], lohot[:, :, :],
                                 tile_f[:, :].unsqueeze(2).broadcast_to([P, NT, CT_]), ALU.mult)
                ve.tensor_tensor(onehot[:, :, :], iota_b[:, :].unsqueeze(1).broadcast_to([P, NT, P]),
                                 slot_hi[:, :].unsqueeze(2).broadcast_to([P, NT, P]), ALU.is_equal
                                 ).then_inc(S.onehot_ready, 1)

            def write_list(q, b):
                ve.wait_ge(S.list_psum, q + 1)
                ve.tensor_copy(listf[:, :], banks[7][:, 64:64 + 2 * CT_]).then_inc(S.listf_ready, 1)
                ve.wait_ge(S.listf_ready, q + 1)
                if not isinstance(q, int) or q >= 2:
                    for x in range(2):
                        ve.wait_ge(o_stored[x], 16 * SUBS * (q - 1))
                ve.scalar_tensor_tensor(lists[:, b, :], listf[:, CT_:], float(P), listf[:, 0:CT_], ALU.mult, ALU.add
                                        ).then_inc(S.list_ready, 1)

            def normalise(k, kb, half, b):
                ve.wait_ge(g_rows[kb], 16 * SUBS * (half + 1))
                wait_after(ve, S.nbT_psum, 2 * k)
                for s in range(SUBS):
                    ve.tensor_scalar(nb[:, s, :], grow[:, kb, s, 0:D], grow[:, kb, s, D:D + 1],
                                     grow[:, kb, s, D + 1:D + 2], ALU.mult, ALU.add).then_inc(S.nb_ready, 1)
                for s in range(SUBS):
                    ve.scalar_tensor_tensor(resb[:, kb, s, :], grow[:, kb, s, 0:D], grow[:, kb, s, D + 2:D + 3],
                                            b2s[:, b, :], ALU.mult, ALU.add).then_inc(S.resb_ready, 1)

            def evac_nbT(k):
                for c in range(KC):
                    ve.wait_ge(S.nbT_psum, 2 * k + c + 1)
                    if c == 0:
                        wait_after(ve, S.mm1_psum, FC * k)
                    ve.tensor_scalar(nbT[:, c, :], banks[5 + c][:, :], vecs[:, FG, c:c + 1], vecs[:, FB, c:c + 1],
                                     ALU.mult, ALU.add).then_inc(S.nbT_ready, 1)

            def finish(k, kb, half, s):
                ve.wait_ge(S.mm2_psum, SUBS * k + s + 1)
                if s == 0:
                    ve.wait_ge(S.resb_ready, SUBS * (k + 1))
                    if not isinstance(half, int) or half >= 1:
                        ve.wait_ge(o_stored[kb], 16 * SUBS * half)
                ve.scalar_tensor_tensor(orow[:, kb, s, :], banks[2 + s % 3][:, 0:D], grow[:, kb, s, D + 3:D + 4],
                                        resb[:, kb, s, :], ALU.add, ALU.add).then_inc(S.final_done, 1)

            begin_search(0)
            for v in range(STEPS):
                count_above(0, v)
                take_digit(0, v)
            mark(0)
            place_tokens(0)
            write_list(0, 0)
            ve.wait_ge(w_loaded[0], 64)
            normalise(0, 0, 0, 0)
            evac_nbT(0)

            def expert(e, half, b, more):
                q, k = e + 1, 2 * e
                if more:
                    begin_search(q)
                    for v in range(FC):
                        count_above(q, v)
                        take_digit(q, v)
                normalise(k + 1, 1, e, b)
                for s in range(SUBS):
                    if more and s < STEPS - FC:
                        count_above(q, FC + s)
                        if s == 1:
                            finish(k, 0, e, 0)
                            evac_nbT(k + 1)
                        if s == 2:
                            finish(k, 0, e, 1)
                        take_digit(q, FC + s)
                if more:
                    mark(q)
                    finish(k, 0, e, 2)
                    finish(k, 0, e, 3)
                    place_tokens(q)
                    write_list(q, 1 - b)
                    if not (isinstance(e, int) and e + 1 >= E):
                        wload(ve, half, b)
                    normalise(k + 2, 0, e + 1, 1 - b)
                    finish(k + 1, 1, e, 0)
                    evac_nbT(k + 2)
                    for s in range(1, SUBS):
                        finish(k + 1, 1, e, s)
                else:
                    finish(k, 0, e, 0)
                    evac_nbT(k + 1)
                    for s in range(1, SUBS):
                        finish(k, 0, e, s)
                    for s in range(SUBS):
                        finish(k + 1, 1, e, s)

            def wload(eng, half, b):
                eng.wait_ge(w_loaded[1 - b], 64 * (half + 1 + b))

            experts(ve, expert)

        @block.tensor
        def _(pe):
            mm = pe.matmul
            pe.wait_ge(S.prep_dve, PREP_IN[0])
            pe.wait_ge(S.wts_loaded, 16 * (8 + len(WCH)))
            pe.wait_ge(S.vec_loaded, 160)
            for n, (wa, wpT, bias) in enumerate(((wk, wkpT, BK), (wq, wqpT, BQ))):
                for k in range(KC):
                    for c in range(KC):
                        x = mm(banks[n][:, k * D:(k + 1) * D], wa[:, c, k * P:(k + 1) * P], wpT[:, c, :],
                               start=(c == 0), stop=(c == KC - 1))
                for k in range(KC):
                    for c in range(KC):
                        x = mm(banks[2][:, 2 * n + k:2 * n + k + 1], wpT[:, c, k * P:(k + 1) * P],
                               vecs[:, bias, c:c + 1], start=(c == 0), stop=(c == KC - 1))
                x.then_inc(S.prep_pe, 1)
            for c in range(KC):
                x = mm(banks[3][:, 0:D], mean_w[:, :], gwo[:, c, :], start=(c == 0), stop=(c == KC - 1))
            x.then_inc(S.prep_pe, 1)
            for c in range(KC):
                x = mm(banks[3][:, D:2 * D], lnb_bc[:, c, :], woT[:, c, :], start=(c == 0), stop=(c == KC - 1))
            x.then_inc(S.prep_pe, 1)
            pe.wait_ge(S.prep_dve, PREP_ALL[0])

            def embed_T(m, s):
                if s == 0:
                    pe.wait_ge(e_rows[m.b], 16 * SUBS * (m.half + 1))
                wait_after(pe, S.eT_ready, SUBS * m.n + s - 1)
                for k, (a, n) in enumerate(WCH):
                    x = pe.transpose(banks[s % 2][0:n, k * P:(k + 1) * P], erow[:, m.b, s, a:a + n], ident[:, :])
                x.then_inc(S.eT_psum, 1)

            def embed_project(m, s):
                pe.wait_ge(S.eT_ready, SUBS * m.n + s + 1)
                if s % 2 == 0:
                    wait_after(pe, S.r1_summed, 2 * m.n + s // 2)
                for k, (a, n) in enumerate(WCH):
                    x = mm(banks[2][:, (s % 2) * D:(s % 2 + 1) * D], eT[0:n, s % 2, k * P:(k + 1) * P], proj[0:n, k, :],
                           start=(k == 0), stop=(k == len(WCH) - 1))
                x.then_inc(S.h0_psum, 1)

            def turn(dst_bank, src, k):
                for s in range(SUBS):
                    x = pe.transpose(banks[dst_bank][:, s * P:(s + 1) * P], src[:, s, k * P:(k + 1) * P], ident[:, :])
                return x

            def memory_T(m):
                pe.wait_ge(S.xhat_ready, SUBS * (m.n + 1))
                for k in range(KC):
                    wait_after(pe, S.bound_ready, 4 * m.n - 2 + 2 * k)
                    turn(3 + k, xhat[:, m.b], k).then_inc(S.xT_psum, 1)

            def project_kqv(m, w):
                for c in range(KC):
                    n = 2 * w + c
                    bank = (5, 3, 4, 5, 3, 4)[n]
                    if n == 0:
                        pe.wait_ge(S.xT_ready, 2 * m.n + 2)
                    if n == 0:
                        wait_after(pe, S.tanh_done, 4 * m.n)
                    if n >= 3:
                        pe.wait_ge(S.tanh_done, 4 * m.n + n - 2)
                    for k in range(KC):
                        x = mm(banks[bank][:, :], wcomb[:, w, k, c * P:(c + 1) * P], xT[:, k, :],
                               start=(k == 0), stop=(k == KC - 1))
                    x.then_inc(S.kqv_psum, 1)

            def retrieved_T(m):
                pe.wait_ge(S.retrieved, m.n + 1)
                for s in range(SUBS):
                    if s % 2 == 0:
                        wait_after(pe, S.nT_ready, 2 * m.n - 1 + s // 2)
                    if s == 2:
                        wait_after(pe, S.scores_saved, m.n)
                    for k in range(KC):
                        x = pe.transpose(banks[6 + s // 2][:, (s % 2) * D + k * P:(s % 2) * D + (k + 1) * P],
                                         ret[:, k, s * P:(s + 1) * P], ident[:, :])
                    x.then_inc(S.rT_psum, 1)

            def mix_out(m, pair):
                pe.wait_ge(S.r_stats, SUBS * m.n + 2 * pair + 2)
                for s in (2 * pair, 2 * pair + 1):
                    for k in range(KC):
                        x = mm(banks[6 + pair][:, (s % 2) * D:(s % 2 + 1) * D], ret[:, k, s * P:(s + 1) * P],
                               wout[:, k, :], start=(k == 0), stop=(k == KC - 1))
                    x.then_inc(S.wo_psum, 1)

            def mix_T(m):
                pe.wait_ge(S.nhat_ready, SUBS * (m.n + 1))
                for k in range(KC):
                    turn(6 + k, nhat, k).then_inc(S.nT_psum, 1)

            def mix_scores(m):
                pe.wait_ge(S.nT_ready, 2 * m.n + 2)
                for s in range(SUBS):
                    for k in range(KC):
                        x = mm(banks[7][:, s * E:(s + 1) * E], nT[:, k, s * P:(s + 1) * P],
                               centT[:, k, :], start=(k == 0), stop=(k == KC - 1))
                x.then_inc(S.scores_psum, 1)

            def step(embed, memory, mix, gather):
                if embed:
                    embed_T(embed, 0)
                    embed_T(embed, 1)
                if mix:
                    retrieved_T(mix)
                if memory:
                    memory_T(memory)
                if embed:
                    embed_project(embed, 0)
                    embed_project(embed, 1)
                if mix:
                    mix_out(mix, 0)
                if memory:
                    project_kqv(memory, 0)
                if embed:
                    embed_T(embed, 2)
                    embed_T(embed, 3)
                if mix:
                    mix_out(mix, 1)
                if memory:
                    project_kqv(memory, 1)
                if embed:
                    embed_project(embed, 2)
                    embed_project(embed, 3)
                if mix:
                    mix_T(mix)
                if mix:
                    mix_scores(mix)
                if memory:
                    project_kqv(memory, 2)

            pipeline(pe, step)

            def count_round(q, v):
                n = 3 if v == 0 else 7
                pe.wait_ge(S.cnt_ready, STEPS * q + v + 1)
                mm(banks[7][:, 0:n], ones[:, :], cnt[:, 0:n], start=True, stop=True).then_inc(S.cnt_psum, 1)

            def rank_round(q):
                pe.wait_ge(S.gteq_ready, 2 * q + 2)
                g = gteq[:, :, :].rearrange("p g n -> p (g n)")
                mm(banks[7][:, 128:128 + 2 * NT], later16[:, :], g, start=True, stop=True)
                mm(banks[7][:, 128 + 2 * NT:128 + 4 * NT], ones16[:, :], g, start=True, stop=True
                   ).then_inc(S.rank_psum, 1)

            def list_round(q):
                pe.wait_ge(S.onehot_ready, q + 1)
                for j in range(NT):
                    x = mm(banks[7][:, 64:64 + 2 * CT_], onehot[:, j, :], tokhot[:, j, :],
                           start=(j == 0), stop=(j == NT - 1))
                x.then_inc(S.list_psum, 1)

            def ffn_T(k, kb):
                pe.wait_ge(S.nb_ready, SUBS * (k + 1))
                wait_after(pe, S.nbT_ready, 2 * k)
                for c in range(KC):
                    turn(5 + c, nb, c).then_inc(S.nbT_psum, 1)

            def up(k, b, f):
                n = FC * k + f
                if f == 0:
                    pe.wait_ge(S.nbT_ready, 2 * k + 2)
                wait_after(pe, S.gelu_done, n - 1)
                for c in range(KC):
                    x = mm(banks[f % 2][:, :], w1s[:, b, c, f * P:(f + 1) * P], nbT[:, c, :],
                           start=(c == 0), stop=(c == KC - 1))
                x.then_inc(S.mm1_psum, 1)

            def down(k, kb, b, s):
                if s == 0:
                    pe.wait_ge(S.gelu_done, FC * (k + 1))
                if s == 0:
                    wait_after(pe, S.final_done, SUBS * k)
                if s == 3:
                    pe.wait_ge(S.final_done, SUBS * k + 1)
                for f in range(FC):
                    x = mm(banks[2 + s % 3][:, 0:D], hT[:, kb, f, s * P:(s + 1) * P],
                           w2s[:, b, f, :], start=(f == 0), stop=(f == FC - 1))
                x.then_inc(S.mm2_psum, 1)

            for v in range(STEPS):
                count_round(0, v)
            rank_round(0)
            list_round(0)
            ffn_T(0, 0)

            def expert(e, half, b, more):
                q, k = e + 1, 2 * e
                pe.wait_ge(w_loaded[b], 64 * (half + 1))
                for f in range(FC):
                    up(k, b, f)
                    if more:
                        count_round(q, f)
                down(k, 0, b, 0)
                if more:
                    count_round(q, FC)
                down(k, 0, b, 1)
                ffn_T(k + 1, 1)
                if more:
                    count_round(q, FC + 1)
                down(k, 0, b, 2)
                if more:
                    count_round(q, FC + 2)
                down(k, 0, b, 3)
                for f in range(FC):
                    up(k + 1, b, f)
                    if more and f == 0:
                        rank_round(q)
                    if more and f == FC - 2:
                        list_round(q)
                down(k + 1, 1, b, 0)
                down(k + 1, 1, b, 1)
                if more:
                    ffn_T(k + 2, 0)
                down(k + 1, 1, b, 2)
                down(k + 1, 1, b, 3)

            experts(pe, expert)


NCONST = [19]
PREP_IN = [8]
PREP_ALL = [0]


def _link(eng, sm, before, count, ins):
    count[0] += 1
    ins.then_inc(sm, 1)
    eng.wait_ge(sm, before + count[0])


def kernel(**inputs):
    import numpy as np
    import concourse.bacc as bacc
    from concourse.bass_utils import run_bass_kernel_spmd as run

    g = {k: np.asarray(v) for k, v in inputs.items()}

    def flat(a):
        return np.ascontiguousarray(a)

    x = g["x"]
    T = x.size
    embs = [g[f"L0_tok_emb{i}"] for i in range(4)]
    width = sum(e.shape[1] for e in embs)
    table = np.zeros((sum(e.shape[0] for e in embs) + 1, width), np.float32)
    r = c = 0
    for e in embs:
        table[r:r + e.shape[0], c:c + e.shape[1]] = e
        r, c = r + e.shape[0], c + e.shape[1]

    def vec(a):
        return flat(a.reshape(-1, P).T)

    a = {
        "tok": flat(x.reshape(T // P, P).T),
        "table": table,
        "projT": flat(np.concatenate([g[f"L0_tok_proj{i}"].T for i in range(4)], axis=0)),
        "wk": flat(g["L0_attn_Wk"]), "wq": flat(g["L0_attn_Wq"]),
        "wkpT": flat(g["L0_attn_Wkp"].T), "wqpT": flat(g["L0_attn_Wqp"].T),
        "wvT": flat(g["L0_attn_Wv"].T), "woT": flat(g["L0_attn_Wo"].T),
        "bo": flat(g["L0_attn_bo"]),
        "bk": vec(g["L0_attn_bk"]), "bv": vec(g["L0_attn_bv"]), "bq": vec(g["L0_attn_bq"]),
        "bkp": vec(g["L0_attn_bkp"]), "bqp": vec(g["L0_attn_bqp"]), "ps": vec(g["L0_attn_phase_scale"]),
        "lg": vec(g["L0_attn_ln_g"]), "lb": vec(g["L0_attn_ln_b"]),
        "fg": vec(g["L0_ffn_ln_g"]), "fb": vec(g["L0_ffn_ln_b"]),
        "centT": flat(g["L0_ffn_centroids"].T),
        "w1": flat(g["L0_ffn_w1"]), "w2": flat(g["L0_ffn_w2"]),
        "b1": flat(g["L0_ffn_b1"].reshape(g["L0_ffn_b1"].shape[0], -1, P).transpose(0, 2, 1)),
        "b2": flat(g["L0_ffn_b2"]),
    }
    nc = bacc.Bacc("TRN2", target_bir_lowering=False, num_devices=1)
    t = {n: nc.dram_tensor(f"in_{n}", v.shape, mybir.dt.from_np(v.dtype), kind="ExternalInput").ap()
         for n, v in a.items()}
    t["out"] = nc.dram_tensor("out_rows", (T, D), F32, kind="ExternalOutput").ap()
    tower(nc, t)
    res = run(nc, [{f"in_{n}": v for n, v in a.items()}], core_ids=[0])
    return res.results[0]["out_rows"].reshape(*x.shape, D)
```

```python
from collections import namedtuple
from contextlib import ExitStack
import math

import concourse.bass as bass
from concourse import mybir

F32 = mybir.dt.float32
BF16 = mybir.dt.bfloat16
I32 = mybir.dt.int32
U32 = mybir.dt.uint32
ALU = mybir.AluOpType
ACT = mybir.ActivationFunctionType
AX = mybir.AxisListType

P = 128
D = 256
KC = D // P
SUBS = 4
MT = SUBS * P
CHUNK = 64
EPS = 1e-5
ROW = D + 4
STEPS = 11
BIG = -3.0e38

Macro = namedtuple("Macro", "n half b")


def tower(nc, t):
    T = t["tok"].shape[0] * t["tok"].shape[1]
    NT = T // P
    NM = T // MT
    V, W = t["table"].shape
    E, _, F = t["w1"].shape
    C = T // E
    FC = F // P
    CT_ = C // P
    WCH = [(a, min(P, W - a)) for a in range(0, W, P)]
    assert C % MT == 0 and C // MT == 2 and W <= 3 * P

    h1_rows = nc.dram_tensor("h1_rows", (T, ROW), F32, kind="Internal").ap()

    ctx = ExitStack()
    with ctx:
        def sb(name, shape, dt=F32):
            return ctx.enter_context(nc.sbuf_tensor(name, shape, dt))

        def sem(name):
            return ctx.enter_context(nc.semaphore(name))

        banks = [ctx.enter_context(nc.psum_tensor(f"bank{i}", [P, 512], F32)) for i in range(8)]

        tok = sb("tok", [P, NT], I32)
        tokf = sb("tokf", [P, NT])
        tokm = sb("tokm", [P, NT])
        row_of = sb("row_of", [P, NT], I32)
        ident = sb("ident", [P, P])
        ones = sb("ones", [P, P])
        mean_w = sb("mean_w", [P, P])
        ones16 = sb("ones16", [P, P], BF16)
        later16 = sb("later16", [P, P], BF16)
        neg_half = sb("neg_half", [P, SUBS])
        eps = sb("eps", [P, SUBS])
        eps_r = sb("eps_r", [P, SUBS])
        plus1 = sb("plus1", [P, SUBS])
        minus1 = sb("minus1", [P, SUBS])
        half_pi = sb("half_pi", [P, 1])
        resets = sb("resets", [P, 2 * MT])
        proj = sb("proj", [P, 3, D])
        work = sb("work", [P, 4, 2, KC * MT])
        raw = work[:, :, :, :].rearrange("p a b m -> p (a b m)")
        wk, wq, wkpT, wqpT, woT, gwo = (raw[:, n * KC * D:(n + 1) * KC * D].rearrange("p (k n) -> p k n", k=KC)
                                        for n in range(6))
        wcomb = sb("wcomb", [P, 3, KC, D])
        wout = sb("wout", [P, KC, D])
        vecs = sb("vecs", [P, 10, KC])
        fbias = sb("fbias", [P, 2, KC])
        turns_of = sb("turns_of", [P, KC])
        lnb_bc = sb("lnb_bc", [P, KC, P])
        bo_bc = sb("bo_bc", [P, D])
        crow = sb("crow", [P, D])
        centT = sb("centT", [P, KC, E])
        BK, BV, BQ, BKP, BQP, PS, LG, LB, FG, FB = range(10)

        cur = sb("cur", [P, SUBS], I32)
        erow = sb("erow", [P, 2, SUBS, 344])
        eT = sb("eT", [P, 2, 3 * P])
        xhat = sb("xhat", [P, 2, SUBS, D])
        r0 = sb("r0", [P, SUBS, D])
        r1 = sb("r1", [P, 2, SUBS, D])
        xT = sb("xT", [P, KC, MT])
        tanh_, frac, sin_, cos_ = (work[:, n] for n in range(4))
        turns = sb("turns", [P, KC * MT], I32)
        fabs = sb("fabs", [P, KC * MT])
        bm = sb("bm", [P, 4, KC * MT])
        bound, mem = bm[:, 0:2], bm[:, 2:4]
        pr = sb("pr", [P, 4, KC * MT])
        part = pr[:, 0:2]
        ret = pr[:, 2:4, :].rearrange("p b (k m) -> p b k m", k=KC)
        hrow = sb("hrow", [P, 2, SUBS, ROW])
        nhat = sb("nhat", [P, SUBS, D])
        nT = sb("nT", [P, KC, MT])
        st_e = sb("st_e", [P, SUBS, 6])
        st_r = sb("st_r", [P, SUBS, 6])
        st_h = sb("st_h", [P, SUBS, 6])
        mv_e = sb("mv_e", [P, SUBS, 2])
        mv_r = sb("mv_r", [P, SUBS, 2])
        mv_h = sb("mv_h", [P, SUBS, 2])
        sc_e = sb("sc_e", [P, 4, SUBS])
        sc_r = sb("sc_r", [P, 2, SUBS])
        sc_h = sb("sc_h", [P, 8, SUBS])
        scoreT = sb("scoreT", [E, MT])
        scores = sb("scores", [P, E, NT])

        w1s = sb("w1s", [P, 2, KC, F])
        w2s = sb("w2s", [P, 2, FC, D])
        b1s = sb("b1s", [P, 2, FC])
        b2s = sb("b2s", [P, 2, D])
        grow = hrow
        nb = nhat
        nbT = nT
        resb = r1
        hT = work[:, :, :, :].rearrange("p a b m -> p (a b m)").rearrange("p (k f m) -> p k f m", k=2, f=FC)
        orow = xhat
        iota_i = sb("iota_i", [P, P], I32)
        iota_b = sb("iota_b", [P, P], BF16)
        part_i = sb("part_i", [P, 1], I32)
        part_f = sb("part_f", [P, 1])
        tile_f = sb("tile_f", [P, NT])
        digits_i = sb("digits_i", [P, 8], I32)
        digits_f = sb("digits_f", [P, 8])
        steps = sb("steps", [P, STEPS, 7], U32)
        first = sb("first", [P, 3])
        flips = sb("flips", [P, 3], U32)
        taken = sb("taken", [P, NT])
        ones64 = sb("ones64", [P, NT])
        masked = sb("masked", [P, NT])
        cand = sb("cand", [P, 7], U32)
        above = sb("above", [P, 7, NT], BF16)
        cnt = sb("cnt", [P, 7])
        flag = sb("flag", [P, 7])
        digit = sb("digit", [P, 1])
        inc = sb("inc", [P, 3], U32)
        thr = sb("thr", [P, 1], U32)
        gteq = sb("gteq", [P, 2, NT], BF16)
        csum = sb("csum", [P, 2, NT])
        rank = sb("rank", [P, 2, NT])
        place = sb("place", [P, NT])
        sel = sb("sel", [P, 2, NT])
        slot = sb("slot", [P, NT], I32)
        slot_hi = sb("slot_hi", [P, NT], I32)
        slot_lo = sb("slot_lo", [P, NT], I32)
        slot_hi16 = sb("slot_hi16", [P, NT], BF16)
        place_of = pr[:, :, :].rearrange("p a m -> p (a m)").bitcast(BF16).rearrange("p (m j) -> p m j", m=P)
        onehot = bm[:, :, :].rearrange("p a m -> p (a m)").bitcast(BF16).rearrange("p (m j) -> p m j", m=P)
        lohot = sb("lohot", [P, NT, CT_], BF16)
        tokhot = sb("tokhot", [P, NT, 2 * CT_], BF16)
        listf = sb("listf", [P, 2 * CT_])
        lists = sb("lists", [P, 2, CT_], I32)

        names = """tok_loaded wts_loaded consts vec_loaded prep_dve prep_pe row_ready cur_ready
            eT_psum eT_ready h0_psum h0_stats h0_meanvar h0_steps h0_scales xhat_ready r1_summed r1_ready
            xT_psum xT_ready kqv_psum tanh_done turn_whole turn_frac turn_abs sin_ready cos_ready
            bound_ready mem_ready mr_cos mi_sin retrieved
            rT_psum r_stats r_meanvar r_steps r_scale wo_psum h1_ready h1_stats h1_meanvar row_steps row_scales
            nhat_ready nT_psum nT_ready scoreT_psum scoreT_ready scores_psum scores_saved pool_go dve_go pe_go
            cand_ready above_ready cnt_ready cnt_psum flag_ready inc_ready thr_ready thr_first
            masked_ready gteq_ready rank_psum place_steps place_of_ready taken_ready onehot_ready list_psum listf_ready list_ready
            nb_ready resb_ready nbT_psum nbT_ready mm1_psum gelu_done mm2_psum final_done sel_init""".split()
        S = namedtuple("Sems", names)(*[sem(n) for n in names])
        e_rows = [sem(f"e_rows{b}") for b in range(2)]
        h_stored = [sem(f"h_stored{b}") for b in range(2)]
        w_loaded = [sem(f"w_loaded{b}") for b in range(2)]
        g_rows = [sem(f"g_rows{b}") for b in range(2)]
        o_stored = [sem(f"o_stored{b}") for b in range(2)]

        block = ctx.enter_context(nc.Block())

        def pipeline(eng, step):
            def at(n, half, b):
                return Macro(n, half, b)

            def static(u):
                return Macro(u, u // 2, u % 2) if 0 <= u < NM else None

            for u in range(4):
                step(static(u), static(u - 1), static(u - 2), static(u - 3), static(u + 1))
            with eng.Fori(0, (NM - 6) // 2) as j:
                for u in (4, 5):
                    step(at(2 * j + u, j + u // 2, u % 2), at(2 * j + u - 1, j + (u - 1) // 2, (u - 1) % 2),
                         at(2 * j + u - 2, j + (u - 2) // 2, u % 2),
                         at(2 * j + u - 3, j + (u - 3) // 2, (u - 3) % 2), at(2 * j + u + 1, j + (u + 1) // 2, (u + 1) % 2))
            for u in range(NM - 2, NM + 3):
                step(static(u), static(u - 1), static(u - 2), static(u - 3), static(u + 1))

        def experts(eng, step):
            step(0, 0, 0, True, True)
            with eng.Fori(0, (E - 4) // 2) as j:
                step(2 * j + 1, j, 1, True, True)
                step(2 * j + 2, j + 1, 0, True, True)
            for e in range(E - 3, E):
                step(e, e // 2, e % 2, e < E - 1, e < E - 2)

        def wait_after(eng, s, v):
            if not isinstance(v, int) or v > 0:
                eng.wait_ge(s, v)

        @block.sync
        def _(sp):
            sp.dma_start(tok[:, :], t["tok"]).then_inc(S.tok_loaded, 16)
            for dst, name in ((wk, "wk"), (wq, "wq"), (wkpT, "wkpT"), (wqpT, "wqpT"), (woT, "woT")):
                sp.dma_start(dst[:, :, :], t[name].rearrange("(k p) n -> p k n", p=P)).then_inc(S.wts_loaded, 16)
            sp.dma_start(wcomb[:, 2, :, :], t["wvT"].rearrange("(k p) n -> p k n", p=P)).then_inc(S.wts_loaded, 16)
            for k, (a, n) in enumerate(WCH):
                sp.dma_start(proj[0:n, k, :], t["projT"][a:a + n, :]).then_inc(S.wts_loaded, 16)
            sp.dma_start(centT[:, :, :], t["centT"].rearrange("(k p) n -> p k n", p=P)).then_inc(S.wts_loaded, 16)
            sp.dma_start(bo_bc[:, :], t["bo"].partition_broadcast(P)).then_inc(S.wts_loaded, 16)

            def load_expert(e, b):
                sp.dma_start(w1s[:, b, :, :], t["w1"][e].rearrange("(k p) f -> p k f", p=P)).then_inc(w_loaded[b], 16)
                sp.dma_start(w2s[:, b, :, :], t["w2"][e].rearrange("(k p) f -> p k f", p=P)).then_inc(w_loaded[b], 16)
                sp.dma_start(b1s[:, b, :], t["b1"][e]).then_inc(w_loaded[b], 16)
                sp.dma_start(b2s[:, b, :], t["b2"][e].partition_broadcast(P)).then_inc(w_loaded[b], 16)

            load_expert(0, 0)
            load_expert(1, 1)

            def store(embed, memory, mix, route, gather):
                if mix:
                    dst = h1_rows[bass.ds(mix.n * MT, MT), :].rearrange("(s p) c -> p s c", p=P)
                    sp.wait_ge(S.row_scales, mix.n + 1)
                    sp.wait_ge(S.row_scales, 1)
                    sp.dma_start(dst, hrow[:, mix.b, :, :]).then_inc(h_stored[mix.b], 16)

            pipeline(sp, store)
            for e in range(2, E):
                sp.wait_ge(S.mm2_psum, 8 * (e - 1))
                sp.wait_ge(S.final_done, 8 * (e - 1))
                load_expert(e, e % 2)
            for b in range(2):
                sp.wait_ge(o_stored[b], 16 * SUBS * E)

        @block.gpsimd
        def _(pl):
            cn = [0]

            def const(ins):
                cn[0] += 1
                ins.then_inc(S.consts, 1)
                return cn[0]

            const(pl.memset(ident[:, :], 0.0))
            const(pl.memset(later16[:, :], -1.0))
            const(pl.memset(resets[:, :], 1.0))
            const(pl.memset(ones[:, :], 1.0))
            const(pl.memset(mean_w[:, :], 1.0 / D))
            const(pl.memset(ones16[:, :], 1.0))
            const(pl.memset(neg_half[:, :], -0.5))
            const(pl.memset(eps[:, :], EPS))
            const(pl.memset(eps_r[:, :], D * EPS))
            const(pl.memset(plus1[:, :], 1.0))
            const(pl.memset(minus1[:, :], -1.0))
            const(pl.memset(half_pi[:, :], math.pi / 2))
            const(pl.memset(ones64[:, :], 1.0))
            const(pl.memset(taken[:, :], 0.0))
            const(pl.iota(iota_i[:, :], pattern=[[1, P]], base=0, channel_multiplier=0))
            const(pl.iota(part_i[:, :], pattern=[[0, 1]], base=0, channel_multiplier=1))
            const(pl.iota(digits_i[:, :], pattern=[[1, 8]], base=1, channel_multiplier=0))
            const(pl.memset(first[:, 0:1], -1.9999998807907104))
            const(pl.memset(first[:, 1:2], 0.0))
            n = const(pl.memset(first[:, 2:3], 2.0))
            pl.wait_ge(S.consts, n)
            const(pl.affine_select(out=ident[:, :], in_=ident[:, :], compare_op=ALU.not_equal, fill=1.0,
                                   base=0, pattern=[[-1, P]], channel_multiplier=1))
            const(pl.affine_select(out=later16[:, :], in_=later16[:, :], compare_op=ALU.is_gt, fill=0.0,
                                   base=0, pattern=[[-1, P]], channel_multiplier=1))
            const(pl.memset(resets[:, 0:2 * MT:CHUNK], 0.0))
            NCONST[0] = cn[0]

            def gather_rows(m):
                if isinstance(m.n, int):
                    src = row_of[:, m.n * SUBS:m.n * SUBS + SUBS]
                else:
                    src = row_of[:, bass.ds(m.n * SUBS, SUBS)]
                wait_after(pl, S.eT_psum, SUBS * (m.n - 1))
                if not isinstance(m.n, int) or m.n >= 2:
                    pl.wait_ge(e_rows[m.b], 16 * SUBS * m.half)
                if not isinstance(m.n, int) or m.n >= 1:
                    pl.wait_ge(e_rows[1 - m.b], 16 * SUBS * (m.half + m.b))
                pl.tensor_copy(cur[:, :], src).then_inc(S.cur_ready, 1)
                pl.wait_ge(S.cur_ready, m.n + 1)
                pl.sem_inc(S.pool_go, 1)
                for s in range(SUBS):
                    pl.indirect_dma_start(erow[:, m.b, s, 0:W], None, t["table"],
                                          bass.IndirectOffsetOnAxis(ap=cur[:, s:s + 1], axis=0)
                                          ).then_inc(e_rows[m.b], 16)

            def pw(out, in_):
                k = in_.shape[1]
                return pl.tensor_tensor(out, in_, neg_half[:, 0:k], ALU.pow)

            def embed_scales(m, pair):
                a = slice(2 * pair, 2 * pair + 2)
                pl.wait_ge(S.h0_meanvar, SUBS * m.n + 2 * pair + 2)
                base = [0]

                def link(ins):
                    _link(pl, S.h0_steps, 6 * m.n + 3 * pair, base, ins)
                link(pl.tensor_tensor(sc_e[:, 0, a], mv_e[:, a, 1], eps[:, 0:2], ALU.add))
                link(pw(sc_e[:, 1, a], sc_e[:, 0, a]))
                link(pl.tensor_tensor(sc_e[:, 2, a], mv_e[:, a, 0], minus1[:, 0:2], ALU.mult))
                pl.tensor_tensor(sc_e[:, 3, a], sc_e[:, 2, a], sc_e[:, 1, a], ALU.mult).then_inc(S.h0_scales, 1)

            def add_crow(m, pair):
                pl.wait_ge(S.r1_summed, 2 * m.n + pair + 1)
                for s in (2 * pair, 2 * pair + 1):
                    pl.tensor_tensor(r1[:, m.b, s, :], r0[:, s, :], crow[:, :], ALU.add
                                     ).then_inc(S.r1_ready, 1)

            def retrieved_scale(m):
                pl.wait_ge(S.r_meanvar, SUBS * (m.n + 1))
                base = [0]
                _link(pl, S.r_steps, m.n, base,
                      pl.tensor_tensor(sc_r[:, 0, :], mv_r[:, :, 1], eps_r[:, :], ALU.add))
                pw(sc_r[:, 1, :], sc_r[:, 0, :]).then_inc(S.r_scale, 1)

            def row_scalars(m):
                pl.wait_ge(S.h1_meanvar, SUBS * (m.n + 1))
                base = [0]
                mean, var = mv_h[:, :, 0], mv_h[:, :, 1]
                ve, rs, sq, v2, v3, rs2, nm = (sc_h[:, n, :] for n in range(7))

                def link(ins):
                    _link(pl, S.row_steps, 9 * m.n, base, ins)
                out = [hrow[:, m.b, :, D + n] for n in range(4)]
                link(pl.tensor_tensor(ve, var, eps[:, :], ALU.add))
                link(pw(rs, ve))
                link(pl.tensor_tensor(sq, rs, rs, ALU.mult))
                link(pl.tensor_tensor(v2, sq, var, ALU.mult))
                link(pl.tensor_tensor(v3, v2, eps[:, :], ALU.add))
                link(pw(rs2, v3))
                link(pl.tensor_tensor(nm, mean, minus1[:, :], ALU.mult))
                if not isinstance(m.n, int) or m.n >= 2:
                    pl.wait_ge(h_stored[m.b], 16 * m.half)
                link(pl.tensor_tensor(out[0], rs, rs2, ALU.mult))
                link(pl.tensor_tensor(out[2], rs, plus1[:, :], ALU.add))
                pl.tensor_tensor(out[3], nm, rs, ALU.mult)
                pl.tensor_tensor(out[1], nm, out[0], ALU.mult).then_inc(S.row_scales, 1)

            def imag_part(m):
                pl.wait_ge(S.mem_ready, 2 * m.n + 2)
                pl.wait_ge(S.sin_ready, 2 * m.n + 2)
                pl.tensor_tensor(part[:, 1, :], mem[:, 1, :], sin_[:, 1, :], ALU.mult).then_inc(S.mi_sin, 1)

            def step(embed, memory, mix, route, gather):
                if embed:
                    embed_scales(embed, 0)
                if memory:
                    add_crow(memory, 0)
                    add_crow(memory, 1)
                if gather:
                    gather_rows(gather)
                if mix:
                    retrieved_scale(mix)
                if embed:
                    embed_scales(embed, 1)
                if memory:
                    imag_part(memory)
                if mix:
                    row_scalars(mix)

            pl.wait_ge(S.row_ready, 4)
            gather_rows(Macro(0, 0, 0))
            pipeline(pl, step)

            def gather(k, b, lst, m, first_of_all=False):
                for s in range(SUBS):
                    pl.indirect_dma_start(grow[:, b, s, :], None, h1_rows,
                                          bass.IndirectOffsetOnAxis(ap=lists[:, lst, m * SUBS + s:m * SUBS + s + 1], axis=0)
                                          ).then_inc(g_rows[b], 16)

            def scatter(k, b, lst):
                pl.wait_ge(S.final_done, SUBS * (k + 1))
                pl.sem_inc(S.pool_go, 1)
                for s in range(SUBS):
                    pl.indirect_dma_start(t["out"], bass.IndirectOffsetOnAxis(ap=lists[:, lst, b * SUBS + s:b * SUBS + s + 1], axis=0),
                                          orow[:, b, s, :], None).then_inc(o_stored[b], 16)

            for b in range(2):
                pl.wait_ge(h_stored[b], 16 * (NM // 2))
            pl.wait_ge(S.list_ready, 1)
            gather(0, 0, 0, 0)

            def expert(e, half, b, more, more2):
                gather(2 * e + 1, 1, b, 1)
                scatter(2 * e, 0, b)
                if more:
                    pl.wait_ge(S.list_ready, e + 2)
                    pl.sem_inc(S.pool_go, 1)
                    gather(2 * e + 2, 0, 1 - b, 0)
                scatter(2 * e + 1, 1, b)

            experts(pl, expert)

        @block.scalar
        def _(ac):
            for n, name in enumerate(("bk", "bv", "bq", "bkp", "bqp", "ps", "lg", "lb", "fg", "fb")):
                ac.dma_start(vecs[:, n, :], t[name]).then_inc(S.vec_loaded, 16)
            ac.preload_act_table_set("silu_and_others")
            ac.wait_ge(S.consts, NCONST[0])

            def ev_eT(m, s):
                ac.wait_ge(S.eT_psum, SUBS * m.n + s + 1)
                wait_after(ac, S.h0_psum, SUBS * m.n + s - 1)
                nfull = 2 * P
                ac.activation(eT[:, s % 2, 0:nfull], banks[s % 2][:, 0:nfull], ACT.Copy)
                ac.activation(eT[0:WCH[2][1], s % 2, nfull:nfull + P], banks[s % 2][0:WCH[2][1], nfull:nfull + P],
                              ACT.Copy).then_inc(S.eT_ready, 1)

            def evac_xT(m):
                for k in range(KC):
                    ac.wait_ge(S.xT_psum, 2 * m.n + k + 1)
                    if k == 0:
                        wait_after(ac, S.kqv_psum, 6 * m.n)
                    ac.activation(xT[:, k, :], banks[3 + k][:, :], ACT.Copy).then_inc(S.xT_ready, 1)

            def make_xhat(m, pair):
                ac.wait_ge(S.h0_scales, 2 * m.n + pair + 1)
                for s in (2 * pair, 2 * pair + 1):
                    ac.activation(xhat[:, m.b, s, :], banks[2][:, (s % 2) * D:(s % 2 + 1) * D], ACT.Identity,
                                  scale=sc_e[:, 1, s:s + 1], bias=sc_e[:, 3, s:s + 1]).then_inc(S.xhat_ready, 1)

            def tanhs(m, kq):
                for c in range(KC):
                    n = 2 * kq + c
                    ac.wait_ge(S.kqv_psum, 6 * m.n + n + 1)
                    if n == 0:
                        wait_after(ac, S.turn_frac, 4 * m.n)
                    ac.activation(tanh_[:, kq, c * MT:(c + 1) * MT], banks[(5, 3, 4, 5)[n]][:, :], ACT.Tanh,
                                  bias=fbias[:, kq, c:c + 1]).then_inc(S.tanh_done, 1)

            def sincos(m, kq):
                if kq == 0:
                    wait_after(ac, S.bound_ready, 4 * m.n)
                else:
                    wait_after(ac, S.retrieved, m.n)
                ac.wait_ge(S.turn_frac, 4 * m.n + 2 * kq + 2)
                ac.activation(sin_[:, kq, :], frac[:, kq, :], ACT.Sin, scale=2 * math.pi).then_inc(S.sin_ready, 1)
                ac.wait_ge(S.turn_abs, 2 * m.n + kq + 1)
                ac.activation(cos_[:, kq, :], fabs[:, :], ACT.Sin, scale=-2 * math.pi,
                              bias=half_pi[:, 0:1]).then_inc(S.cos_ready, 1)

            def copy_scoreT(m):
                ac.wait_ge(S.scoreT_psum, m.n + 1)
                wait_after(ac, S.scores_psum, m.n)
                ac.activation(scoreT[:, :], banks[6][0:E, :], ACT.Copy).then_inc(S.scoreT_ready, 1)

            def make_nhat(m):
                ac.wait_ge(S.row_scales, m.n + 1)
                wait_after(ac, S.nT_psum, 2 * m.n)
                for s in range(SUBS):
                    ac.activation(nhat[:, s, :], hrow[:, m.b, s, 0:D], ACT.Identity,
                                  scale=hrow[:, m.b, s, D:D + 1], bias=hrow[:, m.b, s, D + 1:D + 2]
                                  ).then_inc(S.nhat_ready, 1)

            def step(embed, memory, mix, route, gather):
                if memory:
                    evac_xT(memory)
                if embed:
                    ev_eT(embed, 0)
                    ev_eT(embed, 1)
                if memory:
                    tanhs(memory, 0)
                if route:
                    make_nhat(route)
                if memory:
                    sincos(memory, 0)
                if embed:
                    make_xhat(embed, 0)
                if memory:
                    tanhs(memory, 1)
                if embed:
                    ev_eT(embed, 2)
                    ev_eT(embed, 3)
                if memory:
                    sincos(memory, 1)
                if route:
                    copy_scoreT(route)
                if embed:
                    make_xhat(embed, 1)

            pipeline(ac, step)

            ac.wait_ge(S.wo_psum, SUBS * NM)
            ac.activation(place_of[:, :, :], iota_i[:, :].unsqueeze(2).broadcast_to([P, P, NT]), ACT.Copy
                          ).then_inc(S.place_of_ready, 1)

            def expert(e, half, b, more, more2):
                for m in range(2):
                    for f in range(FC):
                        n = FC * (2 * e + m) + f
                        ac.wait_ge(S.mm1_psum, n + 1)
                        ac.activation(hT[:, m, f, :], banks[f % 2 if FC % 3 else f % 3][:, :], ACT.Gelu_apprx_tanh,
                                      bias=b1s[:, b, f:f + 1]).then_inc(S.gelu_done, 1)

            experts(ac, expert)

        @block.vector
        def _(ve):
            pc = [0]

            def prep(ins):
                pc[0] += 1
                ins.then_inc(S.prep_dve, 1)
                ve.wait_ge(S.prep_dve, pc[0])

            ve.wait_ge(S.tok_loaded, 16)
            rows = V - 1

            def rl(ins, n):
                ins.then_inc(S.row_ready, 1)
                ve.wait_ge(S.row_ready, n)
            rl(ve.tensor_scalar(tokf[:, :], tok[:, :], float(-rows), None, ALU.add), 1)
            rl(ve.tensor_scalar(tokm[:, :], tokf[:, :], float(-rows), None, ALU.is_ge), 2)
            rl(ve.scalar_tensor_tensor(tokm[:, :], tokf[:, :], 0.0, tokm[:, :], ALU.is_lt, ALU.mult), 3)
            ve.tensor_tensor(tokf[:, :], tokf[:, :], tokm[:, :], ALU.mult).then_inc(S.sel_init, 1)
            ve.wait_ge(S.sel_init, 1)
            rl(ve.tensor_scalar(row_of[:, :], tokf[:, :], float(rows), None, ALU.add), 4)

            ve.wait_ge(S.wts_loaded, 16 * (8 + len(WCH)))
            ve.wait_ge(S.vec_loaded, 160)
            ve.wait_ge(S.consts, NCONST[0])
            for k, (a, n) in enumerate(WCH):
                prep(ve.tensor_scalar(proj[0:n, k, :], proj[0:n, k, :], math.sqrt(D), None, ALU.mult))
            prep(ve.tensor_scalar(turns_of[:, :], vecs[:, PS, :], 1.0 / (2 * math.pi), None, ALU.mult))
            for k in range(KC):
                prep(ve.tensor_scalar(gwo[:, k, :], woT[:, k, :], vecs[:, LG, k:k + 1], None, ALU.mult))
                prep(ve.tensor_scalar(lnb_bc[:, k, :], ones[:, :], vecs[:, LB, k:k + 1], None, ALU.mult))
            PREP_IN[0] = pc[0]
            ve.wait_ge(S.prep_pe, 4)
            for n in range(2):
                for k in range(KC):
                    prep(ve.tensor_copy(wcomb[:, n, k, :], banks[n][:, k * D:(k + 1) * D]))
                for k in range(KC):
                    prep(ve.tensor_tensor(fbias[:, n, k:k + 1], banks[2][:, 2 * n + k:2 * n + k + 1],
                                          vecs[:, BKP + n, k:k + 1], ALU.add))
            for k in range(KC):
                prep(ve.tensor_tensor(wout[:, k, :], gwo[:, k, :], banks[3][:, 0:D], ALU.subtract))
            prep(ve.tensor_tensor(crow[:, :], bo_bc[:, :], banks[3][:, D:2 * D], ALU.add))
            prep(ve.tensor_copy(iota_b[:, :], iota_i[:, :]))
            prep(ve.tensor_copy(part_f[:, :], part_i[:, :]))
            prep(ve.tensor_copy(tile_f[:, :], iota_i[:, 0:NT]))
            prep(ve.tensor_copy(digits_f[:, :], digits_i[:, :]))
            for v in range(1, STEPS):
                prep(ve.tensor_scalar(steps[:, v, :], digits_f[:, 0:7], float(1 << (30 - 3 * v)), None, ALU.mult))
            for n, bits in enumerate((1 << 30, 0, 1 << 30)):
                if n != 1:
                    prep(ve.tensor_scalar(flips[:, n:n + 1], digits_f[:, 0:1], float(bits), None, ALU.mult))
            prep(ve.tensor_scalar(flips[:, 1:2].bitcast(I32), digits_f[:, 0:1], -float(1 << 30), None, ALU.mult))
            prep(ve.tensor_scalar(flips[:, 1:2].bitcast(I32), flips[:, 1:2].bitcast(I32), (1 << 31) - 1, None,
                                  ALU.bitwise_xor))
            PREP_ALL[0] = pc[0]

            def stats(m, subs, psum_sem, stat_sem, mv_sem, src, st, mv):
                for s in subs:
                    if s % 2 == 0:
                        ve.wait_ge(psum_sem, SUBS * m.n + s + 2)
                    ve.bn_stats(st[:, s, :], src(s)).then_inc(stat_sem, 1)
                ve.wait_ge(stat_sem, SUBS * m.n + subs[-1] + 1)
                ve.sem_inc(S.dve_go, 1)
                for s in subs:
                    ve.bn_aggr(mv[:, s, :], st[:, s, :]).then_inc(mv_sem, 1)

            def pair_of(bank, s):
                return banks[bank][:, (s % 2) * D:(s % 2 + 1) * D]

            def embed_stats(m, pair):
                stats(m, [2 * pair, 2 * pair + 1], S.h0_psum, S.h0_stats, S.h0_meanvar,
                      lambda s: pair_of(2, s), st_e, mv_e)

            def embed_residual(m, pair):
                ve.wait_ge(S.xhat_ready, SUBS * m.n + 2 * pair + 2)
                wait_after(ve, S.r1_ready, SUBS * (m.n - 1) + 2 * pair + 2)
                ve.tensor_tensor(r0[:, 2 * pair:2 * pair + 2, :],
                                 banks[2][:, :].rearrange("p (s d) -> p s d", s=2),
                                 xhat[:, m.b, 2 * pair:2 * pair + 2, :], ALU.add).then_inc(S.r1_summed, 1)

            def phase_turns(m, kq):
                for c in range(KC):
                    a = slice(c * MT, (c + 1) * MT)
                    n = 2 * kq + c
                    ve.wait_ge(S.tanh_done, 4 * m.n + n + 1)
                    wait_after(ve, S.turn_frac, 4 * m.n + n - 1)
                    ve.tensor_scalar(turns[:, a], tanh_[:, kq, a], turns_of[:, c:c + 1], None, ALU.mult
                                     ).then_inc(S.turn_whole, 1)
                if kq == 0:
                    wait_after(ve, S.sin_ready, 2 * m.n - 1)
                else:
                    wait_after(ve, S.sin_ready, 2 * m.n)
                for c in range(KC):
                    a = slice(c * MT, (c + 1) * MT)
                    n = 2 * kq + c
                    ve.wait_ge(S.turn_whole, 4 * m.n + n + 1)
                    ve.scalar_tensor_tensor(frac[:, kq, a], tanh_[:, kq, a], turns_of[:, c:c + 1], turns[:, a],
                                            ALU.mult, ALU.subtract).then_inc(S.turn_frac, 1)
                ve.wait_ge(S.turn_frac, 4 * m.n + 2 * kq + 2)
                wait_after(ve, S.cos_ready, 2 * m.n + kq)
                ve.tensor_scalar(fabs[:, :].bitcast(I32), frac[:, kq, :].bitcast(I32), (1 << 31) - 1, None,
                                 ALU.bitwise_and).then_inc(S.turn_abs, 1)

            def bind(m):
                ve.wait_ge(S.cos_ready, 2 * m.n + 1)
                for c in range(KC):
                    a = slice(c * MT, (c + 1) * MT)
                    ve.wait_ge(S.kqv_psum, 6 * m.n + 5 + c)
                    for n, trig in enumerate((cos_, sin_)):
                        ve.scalar_tensor_tensor(bound[:, n, a], banks[3 + c][:, :], vecs[:, BV, c:c + 1], trig[:, 0, a],
                                                ALU.add, ALU.mult).then_inc(S.bound_ready, 1)

            def sum_chunks(m):
                ve.wait_ge(S.bound_ready, 4 * m.n + 4)
                wait_after(ve, S.mi_sin, m.n)
                for n in (1, 0):
                    ve.tensor_tensor_scan(mem[:, n, :], resets[:, :], bound[:, n, :], 0.0, ALU.mult, ALU.add
                                          ).then_inc(S.mem_ready, 1)

            def retrieve(m):
                ve.wait_ge(S.mem_ready, 2 * m.n + 2)
                ve.wait_ge(S.cos_ready, 2 * m.n + 2)
                ve.tensor_tensor(part[:, 0, :], mem[:, 0, :], cos_[:, 1, :], ALU.mult).then_inc(S.mr_cos, 1)
                ve.wait_ge(S.mr_cos, m.n + 1)
                ve.wait_ge(S.mi_sin, m.n + 1)
                if not isinstance(m.n, int) or m.n >= 2:
                    ve.wait_ge(S.wo_psum, SUBS * (m.n - 1))
                ve.tensor_tensor(ret[:, m.b, :, :].rearrange("p k m -> p (k m)"), part[:, 0, :], part[:, 1, :], ALU.add
                                 ).then_inc(S.retrieved, 1)

            def retrieved_stats(m):
                stats(m, list(range(SUBS)), S.rT_psum, S.r_stats, S.r_meanvar,
                      lambda s: pair_of(s // 2, s), st_r, mv_r)

            def mix_residual(m, pair):
                ve.wait_ge(S.r_scale, m.n + 1)
                ve.wait_ge(S.r1_ready, SUBS * m.n + 2 * pair + 2)
                if not isinstance(m.n, int) or m.n >= 2:
                    ve.wait_ge(h_stored[m.b], 16 * m.half)
                ve.wait_ge(S.wo_psum, SUBS * m.n + 2 * pair + 2)
                for s in (2 * pair, 2 * pair + 1):
                    ve.scalar_tensor_tensor(hrow[:, m.b, s, 0:D], pair_of(6 + s // 2, s), sc_r[:, 1, s:s + 1],
                                            r1[:, m.b, s, :], ALU.mult, ALU.add).then_inc(S.h1_ready, 1)
                stats(m, [2 * pair, 2 * pair + 1], S.h1_ready, S.h1_stats, S.h1_meanvar,
                      lambda s: hrow[:, m.b, s, 0:D], st_h, mv_h)

            def evac_nT(m):
                for k in range(KC):
                    ve.wait_ge(S.nT_psum, 2 * m.n + k + 1)
                    if k == 0:
                        wait_after(ve, S.scoreT_psum, m.n)
                    ve.tensor_scalar(nT[:, k, :], banks[6 + k][:, :], vecs[:, FG, k:k + 1], vecs[:, FB, k:k + 1],
                                     ALU.mult, ALU.add).then_inc(S.nT_ready, 1)

            def save_scores(m):
                ve.wait_ge(S.scores_psum, m.n + 1)
                dst = scores[:, :, m.n * SUBS:m.n * SUBS + SUBS] if isinstance(m.n, int) else \
                    scores[:, :, bass.ds(m.n * SUBS, SUBS)]
                ve.tensor_copy(dst, banks[7][:, 0:SUBS * E].rearrange("p (s e) -> p e s", e=E)
                               ).then_inc(S.scores_saved, 1)

            def step(embed, memory, mix, route, gather):
                if mix:
                    retrieve(mix)
                if memory:
                    phase_turns(memory, 0)
                if embed:
                    embed_stats(embed, 0)
                    embed_residual(embed, 0)
                if memory:
                    phase_turns(memory, 1)
                if route:
                    evac_nT(route)
                if memory:
                    bind(memory)
                if mix:
                    retrieved_stats(mix)
                if embed:
                    embed_stats(embed, 1)
                if route:
                    save_scores(route)
                if memory:
                    sum_chunks(memory)
                if mix:
                    mix_residual(mix, 0)
                if embed:
                    embed_residual(embed, 1)
                if mix:
                    mix_residual(mix, 1)

            pipeline(ve, step)

            def begin_search(q):
                ve.wait_ge(S.taken_ready, q) if not isinstance(q, int) or q else ve.wait_ge(S.scores_saved, NM)
                src = scores[:, q, :] if isinstance(q, int) else scores[:, bass.ds(q, 1), :].rearrange("p a n -> p (a n)")
                ve.scalar_tensor_tensor(masked[:, :], taken[:, :], BIG, src, ALU.mult, ALU.add
                                        ).then_inc(S.masked_ready, 1)
                ve.wait_ge(S.masked_ready, q + 1)

            def count_above(q, v):
                n = 3 if v == 0 else 7
                if v:
                    ve.tensor_scalar(cand[:, :], steps[:, v, :], thr[:, 0:1], None, ALU.bitwise_xor
                                     ).then_inc(S.cand_ready, 1)
                    ve.wait_ge(S.cand_ready, (STEPS - 1) * q + v)
                c = first[:, :] if v == 0 else cand[:, :].bitcast(F32)
                ve.tensor_tensor(above[:, 0:n, :], masked[:, :].unsqueeze(1).broadcast_to([P, n, NT]),
                                 c.unsqueeze(2).broadcast_to([P, n, NT]), ALU.is_ge).then_inc(S.above_ready, 1)
                ve.wait_ge(S.above_ready, STEPS * q + v + 1)
                ve.tensor_reduce(cnt[:, 0:n], above[:, 0:n, :], AX.X, ALU.add).then_inc(S.cnt_ready, 1)

            def take_digit(q, v):
                ve.wait_ge(S.cnt_psum, STEPS * q + v + 1)
                if v == 0:
                    ve.tensor_scalar(inc[:, :].bitcast(I32), banks[7][:, 0:3], C - 0.5, -1.0, ALU.is_ge, ALU.mult
                                     ).then_inc(S.thr_first, 1)
                    ve.wait_ge(S.thr_first, 3 * q + 1)
                    ve.tensor_tensor(inc[:, :], inc[:, :], flips[:, :], ALU.bitwise_and).then_inc(S.thr_first, 1)
                    ve.wait_ge(S.thr_first, 3 * q + 2)
                    ve.scalar_tensor_tensor(thr[:, :].bitcast(I32), inc[:, 0:1].bitcast(I32), -1,
                                            inc[:, 1:2].bitcast(I32), ALU.bitwise_xor,
                                            ALU.bitwise_xor).then_inc(S.thr_first, 1)
                    ve.wait_ge(S.thr_first, 3 * q + 3)
                    ve.tensor_tensor(thr[:, :], thr[:, :], inc[:, 2:3], ALU.bitwise_xor).then_inc(S.thr_ready, 1)
                else:
                    ve.tensor_scalar(flag[:, :], banks[7][:, 0:7], C - 0.5, None, ALU.is_ge, ALU.add,
                                     accum_out=digit[:, 0:1]).then_inc(S.flag_ready, 1)
                    ve.wait_ge(S.flag_ready, (STEPS - 1) * q + v)
                    ve.tensor_scalar(inc[:, 0:1], digit[:, :], float(1 << (30 - 3 * v)), None, ALU.mult
                                     ).then_inc(S.inc_ready, 1)
                    ve.wait_ge(S.inc_ready, (STEPS - 1) * q + v)
                    ve.tensor_tensor(thr[:, :], thr[:, :], inc[:, 0:1], ALU.bitwise_xor).then_inc(S.thr_ready, 1)
                ve.wait_ge(S.thr_ready, STEPS * q + v + 1)

            def mark(q):
                T_ = thr[:, 0:1].bitcast(F32)
                ve.tensor_scalar(gteq[:, 0, :], masked[:, :], T_, None, ALU.is_gt).then_inc(S.gteq_ready, 1)
                ve.tensor_scalar(gteq[:, 1, :], masked[:, :], T_, None, ALU.is_equal).then_inc(S.gteq_ready, 1)

            def place_tokens(q):
                base = [0]

                def link(ins):
                    _link(ve, S.place_steps, 14 * q, base, ins)
                ve.wait_ge(S.rank_psum, q + 1)
                ve.wait_ge(S.place_of_ready, 1)
                rk = banks[7][:, 128:128 + 4 * NT].rearrange("p (a g n) -> p a g n", a=2, g=2)
                for g in range(2):
                    link(ve.tensor_tensor_scan(csum[:, g, :], ones64[:, :], rk[:, 1, g, :], 0.0, ALU.mult, ALU.add))
                link(ve.tensor_tensor(rank[:, :, :], csum[:, :, :], rk[:, 0, :, :], ALU.add))
                link(ve.tensor_scalar(rank[:, 1, :], rank[:, 1, :], csum[:, 0, NT - 1:NT], None, ALU.add))
                link(ve.tensor_tensor(rank[:, :, :], rank[:, :, :], gteq[:, :, :], ALU.mult))
                link(ve.tensor_tensor(place[:, :], rank[:, 0, :], rank[:, 1, :], ALU.add))
                link(ve.tensor_scalar(sel[:, 0, :], place[:, :], 0.5, None, ALU.is_ge))
                link(ve.scalar_tensor_tensor(sel[:, 1, :], place[:, :], C + 0.5, sel[:, 0, :], ALU.is_le, ALU.mult))
                ve.tensor_tensor(taken[:, :], taken[:, :], sel[:, 1, :], ALU.add).then_inc(S.taken_ready, 1)
                link(ve.scalar_tensor_tensor(place[:, :], sel[:, 1, :], -4.0 * C, place[:, :], ALU.mult, ALU.add))
                link(ve.tensor_scalar(slot[:, :], place[:, :], 4.0 * C - 1.0, None, ALU.add))
                link(ve.tensor_scalar(slot_hi[:, :], slot[:, :], P - 1, None, ALU.bitwise_and))
                link(ve.tensor_copy(slot_hi16[:, :], slot_hi[:, :]))
                link(ve.tensor_scalar(slot_lo[:, :], slot[:, :], int(math.log2(P)), None, ALU.logical_shift_right))
                link(ve.tensor_tensor(lohot[:, :, :], iota_b[:, 0:CT_].unsqueeze(1).broadcast_to([P, NT, CT_]),
                                      slot_lo[:, :].unsqueeze(2).broadcast_to([P, NT, CT_]), ALU.is_equal))
                ve.tensor_scalar(tokhot[:, :, 0:CT_], lohot[:, :, :], part_f[:, 0:1], None, ALU.mult)
                ve.tensor_tensor(tokhot[:, :, CT_:], lohot[:, :, :],
                                 tile_f[:, :].unsqueeze(2).broadcast_to([P, NT, CT_]), ALU.mult)
                ve.tensor_tensor(onehot[:, :, :], place_of[:, :, :],
                                 slot_hi16[:, :].unsqueeze(1).broadcast_to([P, P, NT]), ALU.is_equal
                                 ).then_inc(S.onehot_ready, 1)

            def write_list(q, b):
                ve.wait_ge(S.list_psum, q + 1)
                ve.tensor_copy(listf[:, :], banks[7][:, 64:64 + 2 * CT_]).then_inc(S.listf_ready, 1)
                ve.wait_ge(S.listf_ready, q + 1)
                if not isinstance(q, int) or q >= 2:
                    for x in range(2):
                        ve.wait_ge(o_stored[x], 16 * SUBS * (q - 1))
                ve.scalar_tensor_tensor(lists[:, b, :], listf[:, CT_:], float(P), listf[:, 0:CT_], ALU.mult, ALU.add
                                        ).then_inc(S.list_ready, 1)

            def normalise(k, kb, half):
                ve.wait_ge(g_rows[kb], 16 * SUBS * (half + 1))
                wait_after(ve, S.nbT_psum, 2 * k)
                for s in range(SUBS):
                    ve.tensor_scalar(nb[:, s, :], grow[:, kb, s, 0:D], grow[:, kb, s, D:D + 1],
                                     grow[:, kb, s, D + 1:D + 2], ALU.mult, ALU.add).then_inc(S.nb_ready, 1)

            def prepare_sum(k, kb, b):
                for s in range(SUBS):
                    ve.scalar_tensor_tensor(resb[:, kb, s, :], grow[:, kb, s, 0:D], grow[:, kb, s, D + 2:D + 3],
                                            b2s[:, b, :], ALU.mult, ALU.add).then_inc(S.resb_ready, 1)

            def evac_nbT(k):
                for c in range(KC):
                    ve.wait_ge(S.nbT_psum, 2 * k + c + 1)
                    if c == 0:
                        wait_after(ve, S.mm1_psum, FC * k)
                    ve.tensor_scalar(nbT[:, c, :], banks[5 + c][:, :], vecs[:, FG, c:c + 1], vecs[:, FB, c:c + 1],
                                     ALU.mult, ALU.add).then_inc(S.nbT_ready, 1)

            def finish(k, kb, half, s):
                ve.wait_ge(S.mm2_psum, SUBS * k + s + 1)
                if s == 0:
                    ve.wait_ge(S.resb_ready, SUBS * (k + 1))
                    if not isinstance(half, int) or half >= 1:
                        ve.wait_ge(o_stored[kb], 16 * SUBS * half)
                ve.scalar_tensor_tensor(orow[:, kb, s, :], banks[2 + s % 3][:, 0:D], grow[:, kb, s, D + 3:D + 4],
                                        resb[:, kb, s, :], ALU.add, ALU.add).then_inc(S.final_done, 1)

            def next_round(q, v):
                take_digit(q, v)
                if v < STEPS - 1:
                    count_above(q, v + 1)
                else:
                    mark(q)

            def begin(q):
                begin_search(q)
                count_above(q, 0)

            begin(0)
            for v in range(STEPS):
                next_round(0, v)
            place_tokens(0)
            write_list(0, 0)
            begin(1)
            next_round(1, 0)
            next_round(1, 1)
            ve.wait_ge(w_loaded[0], 64)
            normalise(0, 0, 0)
            evac_nbT(0)
            next_round(1, 2)
            prepare_sum(0, 0, 0)

            def expert(e, half, b, more, more2):
                q, k = e + 1, 2 * e
                if more:
                    next_round(q, 3)
                    next_round(q, 4)
                    next_round(q, 5)
                    next_round(q, 6)
                normalise(k + 1, 1, e)
                for s in range(SUBS):
                    if more:
                        next_round(q, 7 + s)
                    finish(k, 0, e, s)
                    if s == 0:
                        prepare_sum(k + 1, 1, b)
                    if s == 1:
                        evac_nbT(k + 1)
                if more:
                    place_tokens(q)
                    write_list(q, 1 - b)
                    if more2:
                        begin(q + 1)
                    wload(ve, half, b)
                for s in range(SUBS):
                    if more and s == 1:
                        normalise(k + 2, 0, e + 1)
                    if more and s == 2:
                        evac_nbT(k + 2)
                    if more2 and s < 3:
                        next_round(q + 1, s)
                    finish(k + 1, 1, e, s)
                    if more and s == 2:
                        prepare_sum(k + 2, 0, 1 - b)

            def wload(eng, half, b):
                eng.wait_ge(w_loaded[1 - b], 64 * (half + 1 + b))

            experts(ve, expert)

        @block.tensor
        def _(pe):
            mm = pe.matmul
            pe.wait_ge(S.prep_dve, PREP_IN[0])
            pe.wait_ge(S.wts_loaded, 16 * (8 + len(WCH)))
            pe.wait_ge(S.vec_loaded, 160)
            for n, (wa, wpT, bias) in enumerate(((wk, wkpT, BK), (wq, wqpT, BQ))):
                for k in range(KC):
                    for c in range(KC):
                        x = mm(banks[n][:, k * D:(k + 1) * D], wa[:, c, k * P:(k + 1) * P], wpT[:, c, :],
                               start=(c == 0), stop=(c == KC - 1))
                for k in range(KC):
                    for c in range(KC):
                        x = mm(banks[2][:, 2 * n + k:2 * n + k + 1], wpT[:, c, k * P:(k + 1) * P],
                               vecs[:, bias, c:c + 1], start=(c == 0), stop=(c == KC - 1))
                x.then_inc(S.prep_pe, 1)
            for c in range(KC):
                x = mm(banks[3][:, 0:D], mean_w[:, :], gwo[:, c, :], start=(c == 0), stop=(c == KC - 1))
            x.then_inc(S.prep_pe, 1)
            for c in range(KC):
                x = mm(banks[3][:, D:2 * D], lnb_bc[:, c, :], woT[:, c, :], start=(c == 0), stop=(c == KC - 1))
            x.then_inc(S.prep_pe, 1)
            pe.wait_ge(S.prep_dve, PREP_ALL[0])

            def embed_T(m, s):
                if s == 0:
                    pe.wait_ge(e_rows[m.b], 16 * SUBS * (m.half + 1))
                wait_after(pe, S.eT_ready, SUBS * m.n + s - 1)
                for k, (a, n) in enumerate(WCH):
                    x = pe.transpose(banks[s % 2][0:n, k * P:(k + 1) * P], erow[:, m.b, s, a:a + n], ident[:, :])
                x.then_inc(S.eT_psum, 1)

            def embed_project(m, s):
                pe.wait_ge(S.eT_ready, SUBS * m.n + s + 1)
                if s % 2 == 0:
                    wait_after(pe, S.r1_summed, 2 * m.n + s // 2)
                for k, (a, n) in enumerate(WCH):
                    x = mm(banks[2][:, (s % 2) * D:(s % 2 + 1) * D], eT[0:n, s % 2, k * P:(k + 1) * P], proj[0:n, k, :],
                           start=(k == 0), stop=(k == len(WCH) - 1))
                x.then_inc(S.h0_psum, 1)

            def turn(dst_bank, src, k):
                for s in range(SUBS):
                    x = pe.transpose(banks[dst_bank][:, s * P:(s + 1) * P], src[:, s, k * P:(k + 1) * P], ident[:, :])
                return x

            def memory_T(m):
                pe.wait_ge(S.xhat_ready, SUBS * (m.n + 1))
                for k in range(KC):
                    wait_after(pe, S.bound_ready, 4 * m.n - 2 + 2 * k)
                    turn(3 + k, xhat[:, m.b], k).then_inc(S.xT_psum, 1)

            def project_kqv(m, w):
                for c in range(KC):
                    n = 2 * w + c
                    bank = (5, 3, 4, 5, 3, 4)[n]
                    if n == 0:
                        pe.wait_ge(S.xT_ready, 2 * m.n + 2)
                    if n == 0:
                        wait_after(pe, S.tanh_done, 4 * m.n)
                    if n >= 3:
                        pe.wait_ge(S.tanh_done, 4 * m.n + n - 2)
                    for k in range(KC):
                        x = mm(banks[bank][:, :], wcomb[:, w, k, c * P:(c + 1) * P], xT[:, k, :],
                               start=(k == 0), stop=(k == KC - 1))
                    x.then_inc(S.kqv_psum, 1)

            def retrieved_T(m, embed):
                pe.wait_ge(S.retrieved, m.n + 1)
                for s in range(SUBS):
                    if s % 2 == 0 and embed:
                        pe.wait_ge(S.eT_ready, SUBS * embed.n + 3 + s // 2)
                    for k in range(KC):
                        x = pe.transpose(banks[s // 2][:, (s % 2) * D + k * P:(s % 2) * D + (k + 1) * P],
                                         ret[:, m.b, k, s * P:(s + 1) * P], ident[:, :])
                    x.then_inc(S.rT_psum, 1)

            def mix_out(m, pair):
                pe.wait_ge(S.r_stats, SUBS * m.n + 2 * pair + 2)
                if pair == 1:
                    wait_after(pe, S.scores_saved, m.n)
                for s in (2 * pair, 2 * pair + 1):
                    for k in range(KC):
                        x = mm(banks[6 + pair][:, (s % 2) * D:(s % 2 + 1) * D], ret[:, m.b, k, s * P:(s + 1) * P],
                               wout[:, k, :], start=(k == 0), stop=(k == KC - 1))
                    x.then_inc(S.wo_psum, 1)

            def mix_T(m):
                pe.wait_ge(S.nhat_ready, SUBS * (m.n + 1))
                for k in range(KC):
                    turn(6 + k, nhat, k).then_inc(S.nT_psum, 1)

            def route_scores(m):
                pe.wait_ge(S.nT_ready, 2 * m.n + 2)
                for k in range(KC):
                    x = mm(banks[6][0:E, :], centT[:, k, :], nT[:, k, :], start=(k == 0), stop=(k == KC - 1))
                x.then_inc(S.scoreT_psum, 1)

            def route_T(m):
                pe.wait_ge(S.scoreT_ready, m.n + 1)
                pe.sem_inc(S.pe_go, 1)
                for s in range(SUBS):
                    x = pe.transpose(banks[7][:, s * E:(s + 1) * E], scoreT[:, s * P:(s + 1) * P], ident[0:E, 0:E])
                x.then_inc(S.scores_psum, 1)

            def step(embed, memory, mix, route, gather):
                if memory:
                    memory_T(memory)
                if embed:
                    embed_T(embed, 0)
                    embed_T(embed, 1)
                if memory:
                    project_kqv(memory, 0)
                if embed:
                    embed_project(embed, 0)
                    embed_project(embed, 1)
                if memory:
                    project_kqv(memory, 1)
                if route:
                    mix_T(route)
                if embed:
                    embed_T(embed, 2)
                    embed_T(embed, 3)
                if memory:
                    project_kqv(memory, 2)
                if mix:
                    retrieved_T(mix, embed)
                if route:
                    route_scores(route)
                if embed:
                    embed_project(embed, 2)
                    embed_project(embed, 3)
                if route:
                    route_T(route)
                if mix:
                    mix_out(mix, 0)
                    mix_out(mix, 1)

            pipeline(pe, step)

            def count_round(q, v):
                n = 3 if v == 0 else 7
                pe.wait_ge(S.cnt_ready, STEPS * q + v + 1)
                mm(banks[7][:, 0:n], ones[:, :], cnt[:, 0:n], start=True, stop=True).then_inc(S.cnt_psum, 1)

            def rank_round(q):
                pe.wait_ge(S.gteq_ready, 2 * q + 2)
                g = gteq[:, :, :].rearrange("p g n -> p (g n)")
                mm(banks[7][:, 128:128 + 2 * NT], later16[:, :], g, start=True, stop=True)
                mm(banks[7][:, 128 + 2 * NT:128 + 4 * NT], ones16[:, :], g, start=True, stop=True
                   ).then_inc(S.rank_psum, 1)

            def list_round(q):
                pe.wait_ge(S.onehot_ready, q + 1)
                for j in range(NT):
                    x = mm(banks[7][:, 64:64 + 2 * CT_], onehot[:, :, j], tokhot[:, j, :],
                           start=(j == 0), stop=(j == NT - 1))
                x.then_inc(S.list_psum, 1)

            def ffn_T(k, kb):
                pe.wait_ge(S.nb_ready, SUBS * (k + 1))
                wait_after(pe, S.nbT_ready, 2 * k)
                for c in range(KC):
                    turn(5 + c, nb, c).then_inc(S.nbT_psum, 1)

            def up(k, b, f):
                n = FC * k + f
                if f == 0:
                    pe.wait_ge(S.nbT_ready, 2 * k + 2)
                wait_after(pe, S.gelu_done, n - 1)
                for c in range(KC):
                    x = mm(banks[f % 2][:, :], w1s[:, b, c, f * P:(f + 1) * P], nbT[:, c, :],
                           start=(c == 0), stop=(c == KC - 1))
                x.then_inc(S.mm1_psum, 1)

            def down(k, kb, b, s):
                if s == 0:
                    wait_after(pe, S.final_done, SUBS * k)
                if s == 3:
                    pe.wait_ge(S.final_done, SUBS * k + 1)
                for f in range(FC):
                    if s == 0 and f >= FC - 2:
                        pe.wait_ge(S.gelu_done, FC * k + f + 1)
                    x = mm(banks[2 + s % 3][:, 0:D], hT[:, kb, f, s * P:(s + 1) * P],
                           w2s[:, b, f, :], start=(f == 0), stop=(f == FC - 1))
                x.then_inc(S.mm2_psum, 1)

            for v in range(STEPS):
                count_round(0, v)
            rank_round(0)
            list_round(0)
            count_round(1, 0)
            count_round(1, 1)
            ffn_T(0, 0)
            count_round(1, 2)

            def expert(e, half, b, more, more2):
                q, k = e + 1, 2 * e
                pe.wait_ge(w_loaded[b], 64 * (half + 1))
                for f in range(FC):
                    up(k, b, f)
                    if more and f % 2:
                        count_round(q, 3 + f // 2)
                for s in range(SUBS):
                    down(k, 0, b, s)
                    if s == 1:
                        ffn_T(k + 1, 1)
                    if more:
                        count_round(q, 7 + s)
                for f in range(FC):
                    up(k + 1, b, f)
                    if more and f == 0:
                        rank_round(q)
                    if more and f == 7:
                        list_round(q)
                for s in range(SUBS):
                    down(k + 1, 1, b, s)
                    if more and s == 2:
                        ffn_T(k + 2, 0)
                    if more2 and s < 3:
                        count_round(q + 1, s)

            experts(pe, expert)


NCONST = [19]
PREP_IN = [8]
PREP_ALL = [0]


def _link(eng, sm, before, count, ins):
    count[0] += 1
    ins.then_inc(sm, 1)
    eng.wait_ge(sm, before + count[0])


def kernel(**inputs):
    import numpy as np
    import concourse.bacc as bacc
    from concourse.bass_utils import run_bass_kernel_spmd as run

    g = {k: np.asarray(v) for k, v in inputs.items()}

    def flat(a):
        return np.ascontiguousarray(a)

    x = g["x"]
    T = x.size
    embs = [g[f"L0_tok_emb{i}"] for i in range(4)]
    width = sum(e.shape[1] for e in embs)
    table = np.zeros((sum(e.shape[0] for e in embs) + 1, width), np.float32)
    r = c = 0
    for e in embs:
        table[r:r + e.shape[0], c:c + e.shape[1]] = e
        r, c = r + e.shape[0], c + e.shape[1]

    def vec(a):
        return flat(a.reshape(-1, P).T)

    a = {
        "tok": flat(x.reshape(T // P, P).T),
        "table": table,
        "projT": flat(np.concatenate([g[f"L0_tok_proj{i}"].T for i in range(4)], axis=0)),
        "wk": flat(g["L0_attn_Wk"]), "wq": flat(g["L0_attn_Wq"]),
        "wkpT": flat(g["L0_attn_Wkp"].T), "wqpT": flat(g["L0_attn_Wqp"].T),
        "wvT": flat(g["L0_attn_Wv"].T), "woT": flat(g["L0_attn_Wo"].T),
        "bo": flat(g["L0_attn_bo"]),
        "bk": vec(g["L0_attn_bk"]), "bv": vec(g["L0_attn_bv"]), "bq": vec(g["L0_attn_bq"]),
        "bkp": vec(g["L0_attn_bkp"]), "bqp": vec(g["L0_attn_bqp"]), "ps": vec(g["L0_attn_phase_scale"]),
        "lg": vec(g["L0_attn_ln_g"]), "lb": vec(g["L0_attn_ln_b"]),
        "fg": vec(g["L0_ffn_ln_g"]), "fb": vec(g["L0_ffn_ln_b"]),
        "centT": flat(g["L0_ffn_centroids"].T),
        "w1": flat(g["L0_ffn_w1"]), "w2": flat(g["L0_ffn_w2"]),
        "b1": flat(g["L0_ffn_b1"].reshape(g["L0_ffn_b1"].shape[0], -1, P).transpose(0, 2, 1)),
        "b2": flat(g["L0_ffn_b2"]),
    }
    nc = bacc.Bacc("TRN2", target_bir_lowering=False, num_devices=1)
    t = {n: nc.dram_tensor(f"in_{n}", v.shape, mybir.dt.from_np(v.dtype), kind="ExternalInput").ap()
         for n, v in a.items()}
    t["out"] = nc.dram_tensor("out_rows", (T, D), F32, kind="ExternalOutput").ap()
    tower(nc, t)
    res = run(nc, [{f"in_{n}": v for n, v in a.items()}], core_ids=[0])
    return res.results[0]["out_rows"].reshape(*x.shape, D)
```

```python
from collections import namedtuple
from contextlib import ExitStack
import math

import concourse.bass as bass
from concourse import mybir

F32 = mybir.dt.float32
BF16 = mybir.dt.bfloat16
I32 = mybir.dt.int32
F32R = mybir.dt.float32r
U32 = mybir.dt.uint32
ALU = mybir.AluOpType
ACT = mybir.ActivationFunctionType
AX = mybir.AxisListType

P = 128
D = 256
KC = D // P
SUBS = 4
MT = SUBS * P
CHUNK = 64
EPS = 1e-5
ROW = D + 4
STEPS = 11
BIG = -3.0e38

Macro = namedtuple("Macro", "n half b")


def tower(nc, t):
    T = t["tok"].shape[0] * t["tok"].shape[1]
    NT = T // P
    NM = T // MT
    V, W = t["table"].shape
    E, _, F = t["w1"].shape
    C = T // E
    FC = F // P
    CT_ = C // P
    WCH = [(a, min(P, W - a)) for a in range(0, W, P)]
    assert C % MT == 0 and C // MT == 2 and W <= 3 * P

    h1_rows = nc.dram_tensor("h1_rows", (T, ROW), F32, kind="Internal").ap()

    ctx = ExitStack()
    with ctx:
        def sb(name, shape, dt=F32):
            return ctx.enter_context(nc.sbuf_tensor(name, shape, dt))

        def sem(name):
            return ctx.enter_context(nc.semaphore(name))

        banks = [ctx.enter_context(nc.psum_tensor(f"bank{i}", [P, 512], F32)) for i in range(8)]

        tok = sb("tok", [P, NT], I32)
        tokf = sb("tokf", [P, NT])
        tokm = sb("tokm", [P, NT])
        row_of = sb("row_of", [P, NT], I32)
        ident = sb("ident", [P, P])
        ones = sb("ones", [P, P])
        mean_w = sb("mean_w", [P, P])
        ones16 = sb("ones16", [P, P], BF16)
        later16 = sb("later16", [P, P], BF16)
        neg_half = sb("neg_half", [P, SUBS])
        eps = sb("eps", [P, SUBS])
        eps_r = sb("eps_r", [P, SUBS])
        plus1 = sb("plus1", [P, SUBS])
        minus1 = sb("minus1", [P, SUBS])
        half_pi = sb("half_pi", [P, 1])
        vecs = sb("vecs", [P, 10, KC])
        fbias = sb("fbias", [P, 2, KC])
        turns_of = sb("turns_of", [P, KC])
        centT = sb("centT", [P, KC, E])
        BK, BV, BQ, BKP, BQP, PS, LG, LB, FG, FB = range(10)

        xhat = sb("xhat", [P, 2, SUBS, D])
        r1 = sb("r1", [P, 2, SUBS, D])
        hrow = sb("hrow", [P, 2, SUBS, ROW])
        nhat = sb("nhat", [P, SUBS, D])
        nT = sb("nT", [P, KC, MT])
        st_e = sb("st_e", [P, SUBS, 6])
        st_r = sb("st_r", [P, SUBS, 6])
        st_h = sb("st_h", [P, SUBS, 6])
        mv_e = sb("mv_e", [P, SUBS, 2])
        mv_r = sb("mv_r", [P, SUBS, 2])
        mv_h = sb("mv_h", [P, SUBS, 2])
        sc_e = sb("sc_e", [P, 4, SUBS])
        sc_r = sb("sc_r", [P, 2, SUBS])
        sc_h = sb("sc_h", [P, 8, SUBS])
        scoreT = sb("scoreT", [E, MT])
        scores = sb("scores", [P, E, NT])

        w1s = sb("w1s", [P, 2, KC, F])
        w2s = sb("w2s", [P, 2, FC, D])
        b1s = sb("b1s", [P, 2, FC])
        b2s = sb("b2s", [P, 2, D])
        grow = hrow
        nb = nhat
        nbT = nT
        resb = r1
        orow = xhat
        iota_i = sb("iota_i", [P, P], I32)
        iota_b = sb("iota_b", [P, P], BF16)
        part_i = sb("part_i", [P, 1], I32)
        part_f = sb("part_f", [P, 1])
        tile_f = sb("tile_f", [P, NT])
        digits_i = sb("digits_i", [P, 8], I32)
        digits_f = sb("digits_f", [P, 8])
        steps = sb("steps", [P, STEPS, 7], U32)
        first = sb("first", [P, 3])
        flips = sb("flips", [P, 3], U32)
        taken = sb("taken", [P, NT])
        ones64 = sb("ones64", [P, NT])
        masked = sb("masked", [P, NT])
        cand = sb("cand", [P, 7], U32)
        above = sb("above", [P, 7, NT], BF16)
        cnt = sb("cnt", [P, 7], BF16)
        flag = sb("flag", [P, 7])
        digit = sb("digit", [P, 1])
        inc = sb("inc", [P, 3], U32)
        thr = sb("thr", [P, 1], U32)
        gteq = sb("gteq", [P, 2, NT], BF16)
        csum = sb("csum", [P, 2, NT])
        rank = sb("rank", [P, 2, NT])
        place = sb("place", [P, NT])
        sel = sb("sel", [P, 2, NT])
        slot = sb("slot", [P, NT], I32)
        slot_hi = sb("slot_hi", [P, NT], I32)
        slot_lo = sb("slot_lo", [P, NT], I32)
        slot_hi16 = sb("slot_hi16", [P, NT], BF16)
        lohot = sb("lohot", [P, NT, CT_], BF16)
        tokhot = sb("tokhot", [P, NT, 2 * CT_], BF16)
        listf = sb("listf", [P, 2 * CT_])
        lists = sb("lists", [P, 2, CT_], I32)

        phase = ExitStack()

        def sba(name, shape, dt=F32):
            return phase.enter_context(nc.sbuf_tensor(name, shape, dt))

        resets = sba("resets", [P, 2 * MT])
        proj = sba("proj", [P, 3, D])
        work = sba("work", [P, 4, 2, KC * MT])
        raw = work[:, :, :, :].rearrange("p a b m -> p (a b m)")
        wk, wq, wkpT, wqpT, woT, gwo = (raw[:, n * KC * D:(n + 1) * KC * D].rearrange("p (k n) -> p k n", k=KC)
                                        for n in range(6))
        wcomb = sba("wcomb", [P, 3, KC, D])
        wout = sba("wout", [P, KC, D])
        lnb_bc = sba("lnb_bc", [P, KC, P])
        bo_bc = sba("bo_bc", [P, D])
        crow = sba("crow", [P, D])
        cur = sba("cur", [P, SUBS], I32)
        erow = sba("erow", [P, 2, SUBS, 344])
        eT = sba("eT", [P, 2, 3 * P])
        r0 = sba("r0", [P, SUBS, D])
        xT = sba("xT", [P, KC, MT])
        tanh_, frac, sin_, cos_ = (work[:, n] for n in range(4))
        turns = sba("turns", [P, KC * MT], I32)
        fabs = sba("fabs", [P, KC * MT])
        bm = sba("bm", [P, 4, KC * MT])
        bound, mem = bm[:, 0:2], bm[:, 2:4]
        pr = sba("pr", [P, 4, KC * MT])
        part = pr[:, 0:2]
        ret = pr[:, 2:4, :].rearrange("p b (k m) -> p b k m", k=KC)
        phase.close()
        w1hi = sb("w1hi", [P, 2, KC, F], F32R)
        w1lo = sb("w1lo", [P, 2, KC, F], F32R)
        nhi = sb("nhi", [P, KC, MT], F32R)
        nlo = sb("nlo", [P, KC, MT], F32R)
        hT = sb("hT", [P, FC, MT])
        place_of = sb("place_of", [P, P, NT], BF16)
        onehot = sb("onehot", [P, P, NT], BF16)

        names = """tok_loaded proj_loaded wts_loaded consts vec_loaded prep_dve prep_pe row_ready cur_ready
            eT_psum eT_ready h0_psum h0_stats h0_meanvar h0_steps h0_scales xhat_ready r1_summed r1_ready
            xT_psum xT_ready kqv_psum tanh_done turn_whole turn_frac turn_abs sin_ready cos_ready
            bound_ready mem_ready mr_cos mi_sin retrieved
            rT_psum r_stats r_meanvar r_steps r_scale wo_psum h1_ready h1_stats h1_meanvar row_steps row_scales
            nhat_ready nT_psum nT_ready scoreT_psum scoreT_ready scores_psum scores_saved pool_go dve_go pe_go
            cand_ready above_ready cnt_ready cnt_psum flag_ready inc_ready thr_ready thr_first
            masked_ready gteq_ready rank_psum place_steps place_of_ready taken_ready onehot_ready list_psum listf_ready list_ready
            nb_ready resb_ready nbT_psum nbT_ready w1hi_ready w1lo_ready nhi_ready nlo_ready mm1_psum gelu_done mm2_psum final_done sel_init""".split()
        S = namedtuple("Sems", names)(*[sem(n) for n in names])
        e_rows = [sem(f"e_rows{b}") for b in range(2)]
        h_stored = [sem(f"h_stored{b}") for b in range(2)]
        w_loaded = [sem(f"w_loaded{b}") for b in range(2)]
        g_rows = [sem(f"g_rows{b}") for b in range(2)]
        o_stored = [sem(f"o_stored{b}") for b in range(2)]

        block = ctx.enter_context(nc.Block())

        SCALED = len(WCH)
        OPERANDS = SCALED + 1 + 2 * KC
        FOLDED = OPERANDS + 5 * KC + 1
        constants = [0]

        def pipeline(eng, step):
            def at(n, half, b):
                return Macro(n, half, b)

            def static(u):
                return Macro(u, u // 2, u % 2) if 0 <= u < NM else None

            for u in range(4):
                step(static(u), static(u - 1), static(u - 2), static(u - 3), static(u + 1))
            with eng.Fori(0, (NM - 6) // 2) as j:
                for u in (4, 5):
                    step(at(2 * j + u, j + u // 2, u % 2), at(2 * j + u - 1, j + (u - 1) // 2, (u - 1) % 2),
                         at(2 * j + u - 2, j + (u - 2) // 2, u % 2),
                         at(2 * j + u - 3, j + (u - 3) // 2, (u - 3) % 2), at(2 * j + u + 1, j + (u + 1) // 2, (u + 1) % 2))
            for u in range(NM - 2, NM + 3):
                step(static(u), static(u - 1), static(u - 2), static(u - 3), static(u + 1))

        def experts(eng, step):
            step(0, 0, 0, True, True)
            with eng.Fori(0, (E - 4) // 2) as j:
                step(2 * j + 1, j, 1, True, True)
                step(2 * j + 2, j + 1, 0, True, True)
            for e in range(E - 3, E):
                step(e, e // 2, e % 2, e < E - 1, e < E - 2)

        def wait_after(eng, s, v):
            if not isinstance(v, int) or v > 0:
                eng.wait_ge(s, v)

        @block.sync
        def _(sp):
            sp.dma_start(tok[:, :], t["tok"]).then_inc(S.tok_loaded, 16)
            for k, (a, n) in enumerate(WCH):
                sp.dma_start(proj[0:n, k, :], t["projT"][a:a + n, :]).then_inc(S.proj_loaded, 16)
            for dst, name in ((wk, "wk"), (wq, "wq"), (wkpT, "wkpT"), (wqpT, "wqpT"), (woT, "woT")):
                sp.dma_start(dst[:, :, :], t[name].rearrange("(k p) n -> p k n", p=P)).then_inc(S.wts_loaded, 16)
            sp.dma_start(wcomb[:, 2, :, :], t["wvT"].rearrange("(k p) n -> p k n", p=P)).then_inc(S.wts_loaded, 16)
            sp.dma_start(centT[:, :, :], t["centT"].rearrange("(k p) n -> p k n", p=P)).then_inc(S.wts_loaded, 16)
            sp.dma_start(bo_bc[:, :], t["bo"].partition_broadcast(P)).then_inc(S.wts_loaded, 16)

            def load_expert(e, b):
                sp.dma_start(w1s[:, b, :, :], t["w1"][e].rearrange("(k p) f -> p k f", p=P)).then_inc(w_loaded[b], 16)
                sp.dma_start(w2s[:, b, :, :], t["w2"][e].rearrange("(k p) f -> p k f", p=P)).then_inc(w_loaded[b], 16)
                sp.dma_start(b1s[:, b, :], t["b1"][e]).then_inc(w_loaded[b], 16)
                sp.dma_start(b2s[:, b, :], t["b2"][e].partition_broadcast(P)).then_inc(w_loaded[b], 16)

            sp.wait_ge(e_rows[0], 16 * SUBS)
            load_expert(0, 0)
            load_expert(1, 1)

            def store(embed, memory, mix, route, gather):
                if mix:
                    dst = h1_rows[bass.ds(mix.n * MT, MT), :].rearrange("(s p) c -> p s c", p=P)
                    sp.wait_ge(S.row_scales, mix.n + 1)
                    sp.wait_ge(S.row_scales, 1)
                    sp.dma_start(dst, hrow[:, mix.b, :, :]).then_inc(h_stored[mix.b], 16)

            pipeline(sp, store)
            for e in range(2, E):
                sp.wait_ge(S.mm2_psum, 8 * (e - 1))
                sp.wait_ge(S.final_done, 8 * (e - 1))
                load_expert(e, e % 2)
            for b in range(2):
                sp.wait_ge(o_stored[b], 16 * SUBS * E)

        @block.gpsimd
        def _(pl):
            def const(ins):
                constants[0] += 1
                ins.then_inc(S.consts, 1)
                return constants[0]

            const(pl.memset(ident[:, :], 0.0))
            const(pl.memset(later16[:, :], -1.0))
            const(pl.memset(resets[:, :], 1.0))
            const(pl.memset(ones[:, :], 1.0))
            const(pl.memset(mean_w[:, :], 1.0 / D))
            const(pl.memset(ones16[:, :], 1.0))
            const(pl.memset(neg_half[:, :], -0.5))
            const(pl.memset(eps[:, :], EPS))
            const(pl.memset(eps_r[:, :], D * EPS))
            const(pl.memset(plus1[:, :], 1.0))
            const(pl.memset(minus1[:, :], -1.0))
            const(pl.memset(half_pi[:, :], math.pi / 2))
            const(pl.memset(ones64[:, :], 1.0))
            const(pl.memset(taken[:, :], 0.0))
            const(pl.iota(iota_i[:, :], pattern=[[1, P]], base=0, channel_multiplier=0))
            const(pl.iota(part_i[:, :], pattern=[[0, 1]], base=0, channel_multiplier=1))
            const(pl.iota(digits_i[:, :], pattern=[[1, 8]], base=1, channel_multiplier=0))
            const(pl.memset(first[:, 0:1], -1.9999998807907104))
            const(pl.memset(first[:, 1:2], 0.0))
            n = const(pl.memset(first[:, 2:3], 2.0))
            pl.wait_ge(S.consts, n)
            const(pl.affine_select(out=ident[:, :], in_=ident[:, :], compare_op=ALU.not_equal, fill=1.0,
                                   base=0, pattern=[[-1, P]], channel_multiplier=1))
            const(pl.affine_select(out=later16[:, :], in_=later16[:, :], compare_op=ALU.is_gt, fill=0.0,
                                   base=0, pattern=[[-1, P]], channel_multiplier=1))
            const(pl.memset(resets[:, 0:2 * MT:CHUNK], 0.0))

            def gather_rows(m):
                if isinstance(m.n, int):
                    src = row_of[:, m.n * SUBS:m.n * SUBS + SUBS]
                else:
                    src = row_of[:, bass.ds(m.n * SUBS, SUBS)]
                wait_after(pl, S.eT_psum, SUBS * (m.n - 1))
                if not isinstance(m.n, int) or m.n >= 2:
                    pl.wait_ge(e_rows[m.b], 16 * SUBS * m.half)
                if not isinstance(m.n, int) or m.n >= 1:
                    pl.wait_ge(e_rows[1 - m.b], 16 * SUBS * (m.half + m.b))
                pl.tensor_copy(cur[:, :], src).then_inc(S.cur_ready, 1)
                pl.wait_ge(S.cur_ready, m.n + 1)
                pl.sem_inc(S.pool_go, 1)
                for s in range(SUBS):
                    pl.indirect_dma_start(erow[:, m.b, s, 0:W], None, t["table"],
                                          bass.IndirectOffsetOnAxis(ap=cur[:, s:s + 1], axis=0)
                                          ).then_inc(e_rows[m.b], 16)

            def pw(out, in_):
                k = in_.shape[1]
                return pl.tensor_tensor(out, in_, neg_half[:, 0:k], ALU.pow)

            def embed_scales(m, pair):
                a = slice(2 * pair, 2 * pair + 2)
                pl.wait_ge(S.h0_meanvar, SUBS * m.n + 2 * pair + 2)
                base = [0]

                def link(ins):
                    _link(pl, S.h0_steps, 6 * m.n + 3 * pair, base, ins)
                link(pl.tensor_tensor(sc_e[:, 0, a], mv_e[:, a, 1], eps[:, 0:2], ALU.add))
                link(pw(sc_e[:, 1, a], sc_e[:, 0, a]))
                link(pl.tensor_tensor(sc_e[:, 2, a], mv_e[:, a, 0], minus1[:, 0:2], ALU.mult))
                pl.tensor_tensor(sc_e[:, 3, a], sc_e[:, 2, a], sc_e[:, 1, a], ALU.mult).then_inc(S.h0_scales, 1)

            def add_crow(m, pair):
                pl.wait_ge(S.r1_summed, 2 * m.n + pair + 1)
                for s in (2 * pair, 2 * pair + 1):
                    pl.tensor_tensor(r1[:, m.b, s, :], r0[:, s, :], crow[:, :], ALU.add
                                     ).then_inc(S.r1_ready, 1)

            def retrieved_scale(m):
                pl.wait_ge(S.r_meanvar, SUBS * (m.n + 1))
                base = [0]
                _link(pl, S.r_steps, m.n, base,
                      pl.tensor_tensor(sc_r[:, 0, :], mv_r[:, :, 1], eps_r[:, :], ALU.add))
                pw(sc_r[:, 1, :], sc_r[:, 0, :]).then_inc(S.r_scale, 1)

            def row_scalars(m):
                pl.wait_ge(S.h1_meanvar, SUBS * (m.n + 1))
                base = [0]
                mean, var = mv_h[:, :, 0], mv_h[:, :, 1]
                ve, rs, sq, v2, v3, rs2, nm = (sc_h[:, n, :] for n in range(7))

                def link(ins):
                    _link(pl, S.row_steps, 9 * m.n, base, ins)
                out = [hrow[:, m.b, :, D + n] for n in range(4)]
                link(pl.tensor_tensor(ve, var, eps[:, :], ALU.add))
                link(pw(rs, ve))
                link(pl.tensor_tensor(sq, rs, rs, ALU.mult))
                link(pl.tensor_tensor(v2, sq, var, ALU.mult))
                link(pl.tensor_tensor(v3, v2, eps[:, :], ALU.add))
                link(pw(rs2, v3))
                link(pl.tensor_tensor(nm, mean, minus1[:, :], ALU.mult))
                if not isinstance(m.n, int) or m.n >= 2:
                    pl.wait_ge(h_stored[m.b], 16 * m.half)
                link(pl.tensor_tensor(out[0], rs, rs2, ALU.mult))
                link(pl.tensor_tensor(out[2], rs, plus1[:, :], ALU.add))
                pl.tensor_tensor(out[3], nm, rs, ALU.mult)
                pl.tensor_tensor(out[1], nm, out[0], ALU.mult).then_inc(S.row_scales, 1)

            def imag_part(m):
                pl.wait_ge(S.mem_ready, 2 * m.n + 2)
                pl.wait_ge(S.sin_ready, 2 * m.n + 2)
                pl.tensor_tensor(part[:, 1, :], mem[:, 1, :], sin_[:, 1, :], ALU.mult).then_inc(S.mi_sin, 1)

            def step(embed, memory, mix, route, gather):
                if embed:
                    embed_scales(embed, 0)
                if memory:
                    if isinstance(memory.n, int) and memory.n == 0:
                        pl.wait_ge(S.prep_dve, FOLDED)
                    add_crow(memory, 0)
                    add_crow(memory, 1)
                if gather:
                    gather_rows(gather)
                if mix:
                    retrieved_scale(mix)
                if embed:
                    embed_scales(embed, 1)
                if memory:
                    imag_part(memory)
                if mix:
                    row_scalars(mix)

            pl.wait_ge(S.row_ready, 4)
            gather_rows(Macro(0, 0, 0))
            pipeline(pl, step)

            def gather(k, b, lst, m, first_of_all=False):
                for s in range(SUBS):
                    pl.indirect_dma_start(grow[:, b, s, :], None, h1_rows,
                                          bass.IndirectOffsetOnAxis(ap=lists[:, lst, m * SUBS + s:m * SUBS + s + 1], axis=0)
                                          ).then_inc(g_rows[b], 16)

            def scatter(k, b, lst):
                pl.wait_ge(S.final_done, SUBS * (k + 1))
                pl.sem_inc(S.pool_go, 1)
                for s in range(SUBS):
                    pl.indirect_dma_start(t["out"], bass.IndirectOffsetOnAxis(ap=lists[:, lst, b * SUBS + s:b * SUBS + s + 1], axis=0),
                                          orow[:, b, s, :], None).then_inc(o_stored[b], 16)

            def low_w1(e, b, c):
                pl.wait_ge(S.w1hi_ready, 2 * e + c + 1)
                pl.tensor_tensor(w1lo[:, b, c, :], w1s[:, b, c, :], w1hi[:, b, c, :], ALU.subtract
                                 ).then_inc(S.w1lo_ready, 1)

            low_w1(0, 0, 0)
            low_w1(0, 0, 1)
            for b in range(2):
                pl.wait_ge(h_stored[b], 16 * (NM // 2))
            pl.wait_ge(S.list_ready, 1)
            gather(0, 0, 0, 0)

            def expert(e, half, b, more, more2):
                gather(2 * e + 1, 1, b, 1)
                if more:
                    low_w1(e + 1, 1 - b, 0)
                scatter(2 * e, 0, b)
                if more:
                    pl.wait_ge(S.list_ready, e + 2)
                    pl.sem_inc(S.pool_go, 1)
                    gather(2 * e + 2, 0, 1 - b, 0)
                    low_w1(e + 1, 1 - b, 1)
                scatter(2 * e + 1, 1, b)

            experts(pl, expert)

        @block.scalar
        def _(ac):
            ac.dma_start(vecs[:, :, :], t["vecs"]).then_inc(S.vec_loaded, 16)
            ac.preload_act_table_set("silu_and_others")
            ac.wait_ge(S.consts, constants[0])

            def ev_eT(m, s):
                ac.wait_ge(S.eT_psum, SUBS * m.n + s + 1)
                wait_after(ac, S.h0_psum, SUBS * m.n + s - 1)
                nfull = 2 * P
                ac.activation(eT[:, s % 2, 0:nfull], banks[s % 2][:, 0:nfull], ACT.Copy)
                ac.activation(eT[0:WCH[2][1], s % 2, nfull:nfull + P], banks[s % 2][0:WCH[2][1], nfull:nfull + P],
                              ACT.Copy).then_inc(S.eT_ready, 1)

            def evac_xT(m):
                for k in range(KC):
                    ac.wait_ge(S.xT_psum, 2 * m.n + k + 1)
                    if k == 0:
                        wait_after(ac, S.kqv_psum, 6 * m.n)
                    ac.activation(xT[:, k, :], banks[3 + k][:, :], ACT.Copy).then_inc(S.xT_ready, 1)

            def make_xhat(m, pair):
                ac.wait_ge(S.h0_scales, 2 * m.n + pair + 1)
                for s in (2 * pair, 2 * pair + 1):
                    ac.activation(xhat[:, m.b, s, :], banks[2][:, (s % 2) * D:(s % 2 + 1) * D], ACT.Identity,
                                  scale=sc_e[:, 1, s:s + 1], bias=sc_e[:, 3, s:s + 1]).then_inc(S.xhat_ready, 1)

            def tanhs(m, kq):
                for c in range(KC):
                    n = 2 * kq + c
                    ac.wait_ge(S.kqv_psum, 6 * m.n + n + 1)
                    if n == 0:
                        wait_after(ac, S.turn_frac, 4 * m.n)
                    ac.activation(tanh_[:, kq, c * MT:(c + 1) * MT], banks[(5, 3, 4, 5)[n]][:, :], ACT.Tanh,
                                  bias=fbias[:, kq, c:c + 1]).then_inc(S.tanh_done, 1)

            def sincos(m, kq):
                if kq == 0:
                    wait_after(ac, S.bound_ready, 4 * m.n)
                else:
                    wait_after(ac, S.retrieved, m.n)
                ac.wait_ge(S.turn_frac, 4 * m.n + 2 * kq + 2)
                ac.activation(sin_[:, kq, :], frac[:, kq, :], ACT.Sin, scale=2 * math.pi).then_inc(S.sin_ready, 1)
                ac.wait_ge(S.turn_abs, 2 * m.n + kq + 1)
                ac.activation(cos_[:, kq, :], fabs[:, :], ACT.Sin, scale=-2 * math.pi,
                              bias=half_pi[:, 0:1]).then_inc(S.cos_ready, 1)

            def copy_scoreT(m):
                ac.wait_ge(S.scoreT_psum, m.n + 1)
                wait_after(ac, S.scores_psum, m.n)
                ac.activation(scoreT[:, :], banks[6][0:E, :], ACT.Copy).then_inc(S.scoreT_ready, 1)

            def make_nhat(m):
                ac.wait_ge(S.row_scales, m.n + 1)
                wait_after(ac, S.nT_psum, 2 * m.n)
                for s in range(SUBS):
                    ac.activation(nhat[:, s, :], hrow[:, m.b, s, 0:D], ACT.Identity,
                                  scale=hrow[:, m.b, s, D:D + 1], bias=hrow[:, m.b, s, D + 1:D + 2]
                                  ).then_inc(S.nhat_ready, 1)

            def step(embed, memory, mix, route, gather):
                if memory:
                    evac_xT(memory)
                if embed:
                    ev_eT(embed, 0)
                    ev_eT(embed, 1)
                if memory:
                    tanhs(memory, 0)
                if route:
                    make_nhat(route)
                if memory:
                    sincos(memory, 0)
                if embed:
                    make_xhat(embed, 0)
                if memory:
                    tanhs(memory, 1)
                if embed:
                    ev_eT(embed, 2)
                    ev_eT(embed, 3)
                if memory:
                    sincos(memory, 1)
                if route:
                    copy_scoreT(route)
                if embed:
                    make_xhat(embed, 1)

            pipeline(ac, step)

            ac.wait_ge(S.scores_saved, NM)
            ac.activation(place_of[:, :, :], iota_i[:, :].unsqueeze(2).broadcast_to([P, P, NT]), ACT.Copy
                          ).then_inc(S.place_of_ready, 1)

            def round_w1(half, b, c):
                if c == 0:
                    ac.wait_ge(w_loaded[b], 64 * (half + 1))
                ac.activation(w1hi[:, b, c, :], w1s[:, b, c, :], ACT.Copy).then_inc(S.w1hi_ready, 1)

            def normalise(k, kb, half):
                ac.wait_ge(g_rows[kb], 16 * SUBS * (half + 1))
                wait_after(ac, S.nbT_psum, 2 * k)
                for s in range(SUBS):
                    ac.activation(nb[:, s, :], grow[:, kb, s, 0:D], ACT.Identity, scale=grow[:, kb, s, D:D + 1],
                                  bias=grow[:, kb, s, D + 1:D + 2]).then_inc(S.nb_ready, 1)

            def evac_nbT(k, first):
                for c in range(KC):
                    ac.wait_ge(S.nbT_psum, 2 * k + c + 1)
                    if c == 0 and not first:
                        ac.wait_ge(S.nlo_ready, 2 * k)
                    ac.activation(nbT[:, c, :], banks[5 + c][:, :], ACT.Identity, scale=vecs[:, FG, c:c + 1],
                                  bias=vecs[:, FB, c:c + 1]).then_inc(S.nbT_ready, 1)
                for c in range(KC):
                    ac.wait_ge(S.nbT_ready, 2 * k + c + 1)
                    if c == 0 and not first:
                        ac.wait_ge(S.mm1_psum, FC * k)
                    ac.activation(nhi[:, c, :], nbT[:, c, :], ACT.Copy).then_inc(S.nhi_ready, 1)

            def gelus(k, b):
                for f in range(FC):
                    ac.wait_ge(S.mm1_psum, FC * k + f + 1)
                    ac.activation(hT[:, f, :], banks[f % 2][:, :], ACT.Gelu_apprx_tanh,
                                  bias=b1s[:, b, f:f + 1]).then_inc(S.gelu_done, 1)

            round_w1(0, 0, 0)
            round_w1(0, 0, 1)
            normalise(0, 0, 0)
            evac_nbT(0, True)

            def expert(e, half, b, more, more2):
                gelus(2 * e, b)
                if more:
                    round_w1(half + b, 1 - b, 0)
                normalise(2 * e + 1, 1, e)
                evac_nbT(2 * e + 1, False)
                gelus(2 * e + 1, b)
                if more:
                    round_w1(half + b, 1 - b, 1)
                    normalise(2 * e + 2, 0, e + 1)
                    evac_nbT(2 * e + 2, False)

            experts(ac, expert)

        @block.vector
        def _(ve):
            pc = [0]

            def prep(ins):
                pc[0] += 1
                ins.then_inc(S.prep_dve, 1)
                ve.wait_ge(S.prep_dve, pc[0])

            ve.wait_ge(S.tok_loaded, 16)
            rows = V - 1

            def rl(ins, n):
                ins.then_inc(S.row_ready, 1)
                ve.wait_ge(S.row_ready, n)
            rl(ve.tensor_scalar(tokf[:, :], tok[:, :], float(-rows), None, ALU.add), 1)
            rl(ve.tensor_scalar(tokm[:, :], tokf[:, :], float(-rows), None, ALU.is_ge), 2)
            rl(ve.scalar_tensor_tensor(tokm[:, :], tokf[:, :], 0.0, tokm[:, :], ALU.is_lt, ALU.mult), 3)
            ve.tensor_tensor(tokf[:, :], tokf[:, :], tokm[:, :], ALU.mult).then_inc(S.sel_init, 1)
            ve.wait_ge(S.sel_init, 1)
            rl(ve.tensor_scalar(row_of[:, :], tokf[:, :], float(rows), None, ALU.add), 4)

            def scale_projection():
                ve.wait_ge(S.proj_loaded, 16 * len(WCH))
                for k, (a, n) in enumerate(WCH):
                    prep(ve.tensor_scalar(proj[0:n, k, :], proj[0:n, k, :], math.sqrt(D), None, ALU.mult))

            def prepare_operands():
                ve.wait_ge(S.wts_loaded, 16 * 8)
                ve.wait_ge(S.vec_loaded, 16)
                ve.wait_ge(S.consts, constants[0])
                prep(ve.tensor_scalar(turns_of[:, :], vecs[:, PS, :], 1.0 / (2 * math.pi), None, ALU.mult))
                for k in range(KC):
                    prep(ve.tensor_scalar(gwo[:, k, :], woT[:, k, :], vecs[:, LG, k:k + 1], None, ALU.mult))
                    prep(ve.tensor_scalar(lnb_bc[:, k, :], ones[:, :], vecs[:, LB, k:k + 1], None, ALU.mult))

            def save_folded():
                ve.wait_ge(S.prep_pe, 4)
                for n in range(2):
                    for k in range(KC):
                        prep(ve.tensor_copy(wcomb[:, n, k, :], banks[4 + n][:, k * D:(k + 1) * D]))
                    for k in range(KC):
                        prep(ve.tensor_tensor(fbias[:, n, k:k + 1], banks[6][:, 2 * n + k:2 * n + k + 1],
                                              vecs[:, BKP + n, k:k + 1], ALU.add))
                for k in range(KC):
                    prep(ve.tensor_tensor(wout[:, k, :], gwo[:, k, :], banks[3][:, 0:D], ALU.subtract))
                prep(ve.tensor_tensor(crow[:, :], bo_bc[:, :], banks[3][:, D:2 * D], ALU.add))

            def search_constants():
                prep(ve.tensor_copy(iota_b[:, :], iota_i[:, :]))
                prep(ve.tensor_copy(part_f[:, :], part_i[:, :]))
                prep(ve.tensor_copy(tile_f[:, :], iota_i[:, 0:NT]))
                prep(ve.tensor_copy(digits_f[:, :], digits_i[:, :]))
                for v in range(1, STEPS):
                    prep(ve.tensor_scalar(steps[:, v, :], digits_f[:, 0:7], float(1 << (30 - 3 * v)), None, ALU.mult))
                for n, bits in enumerate((1 << 30, 0, 1 << 30)):
                    if n != 1:
                        prep(ve.tensor_scalar(flips[:, n:n + 1], digits_f[:, 0:1], float(bits), None, ALU.mult))
                prep(ve.tensor_scalar(flips[:, 1:2].bitcast(I32), digits_f[:, 0:1], -float(1 << 30), None, ALU.mult))
                prep(ve.tensor_scalar(flips[:, 1:2].bitcast(I32), flips[:, 1:2].bitcast(I32), (1 << 31) - 1, None,
                                      ALU.bitwise_xor))

            def stats(m, subs, psum_sem, stat_sem, mv_sem, src, st, mv):
                for s in subs:
                    if s % 2 == 0:
                        ve.wait_ge(psum_sem, SUBS * m.n + s + 2)
                    ve.bn_stats(st[:, s, :], src(s)).then_inc(stat_sem, 1)
                ve.wait_ge(stat_sem, SUBS * m.n + subs[-1] + 1)
                ve.sem_inc(S.dve_go, 1)
                for s in subs:
                    ve.bn_aggr(mv[:, s, :], st[:, s, :]).then_inc(mv_sem, 1)

            def pair_of(bank, s):
                return banks[bank][:, (s % 2) * D:(s % 2 + 1) * D]

            def embed_stats(m, pair):
                stats(m, [2 * pair, 2 * pair + 1], S.h0_psum, S.h0_stats, S.h0_meanvar,
                      lambda s: pair_of(2, s), st_e, mv_e)

            def embed_residual(m, pair):
                ve.wait_ge(S.xhat_ready, SUBS * m.n + 2 * pair + 2)
                wait_after(ve, S.r1_ready, SUBS * (m.n - 1) + 2 * pair + 2)
                ve.tensor_tensor(r0[:, 2 * pair:2 * pair + 2, :],
                                 banks[2][:, :].rearrange("p (s d) -> p s d", s=2),
                                 xhat[:, m.b, 2 * pair:2 * pair + 2, :], ALU.add).then_inc(S.r1_summed, 1)

            def phase_turns(m, kq):
                for c in range(KC):
                    a = slice(c * MT, (c + 1) * MT)
                    n = 2 * kq + c
                    ve.wait_ge(S.tanh_done, 4 * m.n + n + 1)
                    wait_after(ve, S.turn_frac, 4 * m.n + n - 1)
                    ve.tensor_scalar(turns[:, a], tanh_[:, kq, a], turns_of[:, c:c + 1], None, ALU.mult
                                     ).then_inc(S.turn_whole, 1)
                if kq == 0:
                    wait_after(ve, S.sin_ready, 2 * m.n - 1)
                else:
                    wait_after(ve, S.sin_ready, 2 * m.n)
                for c in range(KC):
                    a = slice(c * MT, (c + 1) * MT)
                    n = 2 * kq + c
                    ve.wait_ge(S.turn_whole, 4 * m.n + n + 1)
                    ve.scalar_tensor_tensor(frac[:, kq, a], tanh_[:, kq, a], turns_of[:, c:c + 1], turns[:, a],
                                            ALU.mult, ALU.subtract).then_inc(S.turn_frac, 1)
                ve.wait_ge(S.turn_frac, 4 * m.n + 2 * kq + 2)
                wait_after(ve, S.cos_ready, 2 * m.n + kq)
                ve.tensor_scalar(fabs[:, :].bitcast(I32), frac[:, kq, :].bitcast(I32), (1 << 31) - 1, None,
                                 ALU.bitwise_and).then_inc(S.turn_abs, 1)

            def bind(m):
                ve.wait_ge(S.cos_ready, 2 * m.n + 1)
                for c in range(KC):
                    a = slice(c * MT, (c + 1) * MT)
                    ve.wait_ge(S.kqv_psum, 6 * m.n + 5 + c)
                    for n, trig in enumerate((cos_, sin_)):
                        ve.scalar_tensor_tensor(bound[:, n, a], banks[3 + c][:, :], vecs[:, BV, c:c + 1], trig[:, 0, a],
                                                ALU.add, ALU.mult).then_inc(S.bound_ready, 1)

            def sum_chunks(m):
                ve.wait_ge(S.bound_ready, 4 * m.n + 4)
                wait_after(ve, S.mi_sin, m.n)
                for n in (1, 0):
                    ve.tensor_tensor_scan(mem[:, n, :], resets[:, :], bound[:, n, :], 0.0, ALU.mult, ALU.add
                                          ).then_inc(S.mem_ready, 1)

            def retrieve(m):
                ve.wait_ge(S.mem_ready, 2 * m.n + 2)
                ve.wait_ge(S.cos_ready, 2 * m.n + 2)
                ve.tensor_tensor(part[:, 0, :], mem[:, 0, :], cos_[:, 1, :], ALU.mult).then_inc(S.mr_cos, 1)
                ve.wait_ge(S.mr_cos, m.n + 1)
                ve.wait_ge(S.mi_sin, m.n + 1)
                if not isinstance(m.n, int) or m.n >= 2:
                    ve.wait_ge(S.wo_psum, SUBS * (m.n - 1))
                ve.tensor_tensor(ret[:, m.b, :, :].rearrange("p k m -> p (k m)"), part[:, 0, :], part[:, 1, :], ALU.add
                                 ).then_inc(S.retrieved, 1)

            def retrieved_stats(m):
                stats(m, list(range(SUBS)), S.rT_psum, S.r_stats, S.r_meanvar,
                      lambda s: pair_of(s // 2, s), st_r, mv_r)

            def mix_residual(m, pair):
                ve.wait_ge(S.r_scale, m.n + 1)
                ve.wait_ge(S.r1_ready, SUBS * m.n + 2 * pair + 2)
                if not isinstance(m.n, int) or m.n >= 2:
                    ve.wait_ge(h_stored[m.b], 16 * m.half)
                ve.wait_ge(S.wo_psum, SUBS * m.n + 2 * pair + 2)
                for s in (2 * pair, 2 * pair + 1):
                    ve.scalar_tensor_tensor(hrow[:, m.b, s, 0:D], pair_of(6 + s // 2, s), sc_r[:, 1, s:s + 1],
                                            r1[:, m.b, s, :], ALU.mult, ALU.add).then_inc(S.h1_ready, 1)
                stats(m, [2 * pair, 2 * pair + 1], S.h1_ready, S.h1_stats, S.h1_meanvar,
                      lambda s: hrow[:, m.b, s, 0:D], st_h, mv_h)

            def evac_nT(m):
                for k in range(KC):
                    ve.wait_ge(S.nT_psum, 2 * m.n + k + 1)
                    if k == 0:
                        wait_after(ve, S.scoreT_psum, m.n)
                    ve.tensor_scalar(nT[:, k, :], banks[6 + k][:, :], vecs[:, FG, k:k + 1], vecs[:, FB, k:k + 1],
                                     ALU.mult, ALU.add).then_inc(S.nT_ready, 1)

            def save_scores(m):
                ve.wait_ge(S.scores_psum, m.n + 1)
                dst = scores[:, :, m.n * SUBS:m.n * SUBS + SUBS] if isinstance(m.n, int) else \
                    scores[:, :, bass.ds(m.n * SUBS, SUBS)]
                ve.tensor_copy(dst, banks[7][:, 0:SUBS * E].rearrange("p (s e) -> p e s", e=E)
                               ).then_inc(S.scores_saved, 1)

            def step(embed, memory, mix, route, gather):
                if mix:
                    retrieve(mix)
                if memory:
                    phase_turns(memory, 0)
                if embed and not memory:
                    prepare_operands()
                if embed:
                    embed_stats(embed, 0)
                    embed_residual(embed, 0)
                if embed and not memory:
                    save_folded()
                if memory:
                    phase_turns(memory, 1)
                if route:
                    evac_nT(route)
                if memory:
                    bind(memory)
                if mix:
                    retrieved_stats(mix)
                if embed:
                    embed_stats(embed, 1)
                if route:
                    save_scores(route)
                if memory:
                    sum_chunks(memory)
                if mix:
                    mix_residual(mix, 0)
                if embed:
                    embed_residual(embed, 1)
                if mix:
                    mix_residual(mix, 1)
                if memory and not embed:
                    search_constants()

            scale_projection()
            pipeline(ve, step)

            def begin_search(q):
                ve.wait_ge(S.taken_ready, q) if not isinstance(q, int) or q else ve.wait_ge(S.scores_saved, NM)
                src = scores[:, q, :] if isinstance(q, int) else scores[:, bass.ds(q, 1), :].rearrange("p a n -> p (a n)")
                ve.scalar_tensor_tensor(masked[:, :], taken[:, :], BIG, src, ALU.mult, ALU.add
                                        ).then_inc(S.masked_ready, 1)
                ve.wait_ge(S.masked_ready, q + 1)

            def count_above(q, v):
                n = 3 if v == 0 else 7
                if v:
                    ve.tensor_scalar(cand[:, :], steps[:, v, :], thr[:, 0:1], None, ALU.bitwise_xor
                                     ).then_inc(S.cand_ready, 1)
                    ve.wait_ge(S.cand_ready, (STEPS - 1) * q + v)
                c = first[:, :] if v == 0 else cand[:, :].bitcast(F32)
                ve.tensor_tensor(above[:, 0:n, :], masked[:, :].unsqueeze(1).broadcast_to([P, n, NT]),
                                 c.unsqueeze(2).broadcast_to([P, n, NT]), ALU.is_ge).then_inc(S.above_ready, 1)
                ve.wait_ge(S.above_ready, STEPS * q + v + 1)
                with nc.allow_low_precision(reason="counts up to NT are exact in bfloat16"):
                    ve.tensor_reduce(cnt[:, 0:n], above[:, 0:n, :], AX.X, ALU.add).then_inc(S.cnt_ready, 1)

            def take_digit(q, v):
                ve.wait_ge(S.cnt_psum, STEPS * q + v + 1)
                if v == 0:
                    ve.tensor_scalar(inc[:, :].bitcast(I32), banks[7][:, 0:3], C - 0.5, -1.0, ALU.is_ge, ALU.mult
                                     ).then_inc(S.thr_first, 1)
                    ve.wait_ge(S.thr_first, 3 * q + 1)
                    ve.tensor_tensor(inc[:, :], inc[:, :], flips[:, :], ALU.bitwise_and).then_inc(S.thr_first, 1)
                    ve.wait_ge(S.thr_first, 3 * q + 2)
                    ve.scalar_tensor_tensor(thr[:, :].bitcast(I32), inc[:, 0:1].bitcast(I32), -1,
                                            inc[:, 1:2].bitcast(I32), ALU.bitwise_xor,
                                            ALU.bitwise_xor).then_inc(S.thr_first, 1)
                    ve.wait_ge(S.thr_first, 3 * q + 3)
                    ve.tensor_tensor(thr[:, :], thr[:, :], inc[:, 2:3], ALU.bitwise_xor).then_inc(S.thr_ready, 1)
                else:
                    ve.tensor_scalar(flag[:, :], banks[7][:, 0:7], C - 0.5, None, ALU.is_ge, ALU.add,
                                     accum_out=digit[:, 0:1]).then_inc(S.flag_ready, 1)
                    ve.wait_ge(S.flag_ready, (STEPS - 1) * q + v)
                    ve.tensor_scalar(inc[:, 0:1], digit[:, :], float(1 << (30 - 3 * v)), None, ALU.mult
                                     ).then_inc(S.inc_ready, 1)
                    ve.wait_ge(S.inc_ready, (STEPS - 1) * q + v)
                    ve.tensor_tensor(thr[:, :], thr[:, :], inc[:, 0:1], ALU.bitwise_xor).then_inc(S.thr_ready, 1)
                ve.wait_ge(S.thr_ready, STEPS * q + v + 1)

            def mark(q):
                T_ = thr[:, 0:1].bitcast(F32)
                ve.tensor_scalar(gteq[:, 0, :], masked[:, :], T_, None, ALU.is_gt).then_inc(S.gteq_ready, 1)
                ve.tensor_scalar(gteq[:, 1, :], masked[:, :], T_, None, ALU.is_equal).then_inc(S.gteq_ready, 1)

            def place_tokens(q):
                base = [0]

                def link(ins):
                    _link(ve, S.place_steps, 14 * q, base, ins)
                ve.wait_ge(S.rank_psum, q + 1)
                ve.wait_ge(S.place_of_ready, 1)
                rk = banks[7][:, 128:128 + 4 * NT].rearrange("p (a g n) -> p a g n", a=2, g=2)
                for g in range(2):
                    link(ve.tensor_tensor_scan(csum[:, g, :], ones64[:, :], rk[:, 1, g, :], 0.0, ALU.mult, ALU.add))
                link(ve.tensor_tensor(rank[:, :, :], csum[:, :, :], rk[:, 0, :, :], ALU.add))
                link(ve.tensor_scalar(rank[:, 1, :], rank[:, 1, :], csum[:, 0, NT - 1:NT], None, ALU.add))
                link(ve.tensor_tensor(rank[:, :, :], rank[:, :, :], gteq[:, :, :], ALU.mult))
                link(ve.tensor_tensor(place[:, :], rank[:, 0, :], rank[:, 1, :], ALU.add))
                link(ve.tensor_scalar(sel[:, 0, :], place[:, :], 0.5, None, ALU.is_ge))
                link(ve.scalar_tensor_tensor(sel[:, 1, :], place[:, :], C + 0.5, sel[:, 0, :], ALU.is_le, ALU.mult))
                ve.tensor_tensor(taken[:, :], taken[:, :], sel[:, 1, :], ALU.add).then_inc(S.taken_ready, 1)
                link(ve.scalar_tensor_tensor(place[:, :], sel[:, 1, :], -4.0 * C, place[:, :], ALU.mult, ALU.add))
                link(ve.tensor_scalar(slot[:, :], place[:, :], 4.0 * C - 1.0, None, ALU.add))
                link(ve.tensor_scalar(slot_hi[:, :], slot[:, :], P - 1, None, ALU.bitwise_and))
                link(ve.tensor_copy(slot_hi16[:, :], slot_hi[:, :]))
                link(ve.tensor_scalar(slot_lo[:, :], slot[:, :], int(math.log2(P)), None, ALU.logical_shift_right))
                link(ve.tensor_tensor(lohot[:, :, :], iota_b[:, 0:CT_].unsqueeze(1).broadcast_to([P, NT, CT_]),
                                      slot_lo[:, :].unsqueeze(2).broadcast_to([P, NT, CT_]), ALU.is_equal))
                ve.tensor_scalar(tokhot[:, :, 0:CT_], lohot[:, :, :], part_f[:, 0:1], None, ALU.mult)
                ve.tensor_tensor(tokhot[:, :, CT_:], lohot[:, :, :],
                                 tile_f[:, :].unsqueeze(2).broadcast_to([P, NT, CT_]), ALU.mult)
                ve.tensor_tensor(onehot[:, :, :], place_of[:, :, :],
                                 slot_hi16[:, :].unsqueeze(1).broadcast_to([P, P, NT]), ALU.is_equal
                                 ).then_inc(S.onehot_ready, 1)

            def write_list(q, b):
                ve.wait_ge(S.list_psum, q + 1)
                ve.tensor_copy(listf[:, :], banks[7][:, 64:64 + 2 * CT_]).then_inc(S.listf_ready, 1)
                ve.wait_ge(S.listf_ready, q + 1)
                if not isinstance(q, int) or q >= 2:
                    for x in range(2):
                        ve.wait_ge(o_stored[x], 16 * SUBS * (q - 1))
                ve.scalar_tensor_tensor(lists[:, b, :], listf[:, CT_:], float(P), listf[:, 0:CT_], ALU.mult, ALU.add
                                        ).then_inc(S.list_ready, 1)

            def prepare_sum(k, kb, b):
                ve.wait_ge(S.nb_ready, SUBS * (k + 1))
                for s in range(SUBS):
                    ve.scalar_tensor_tensor(resb[:, kb, s, :], grow[:, kb, s, 0:D], grow[:, kb, s, D + 2:D + 3],
                                            b2s[:, b, :], ALU.mult, ALU.add).then_inc(S.resb_ready, 1)

            def low_nbT(k):
                for c in range(KC):
                    ve.wait_ge(S.nhi_ready, 2 * k + c + 1)
                    ve.tensor_tensor(nlo[:, c, :], nbT[:, c, :], nhi[:, c, :], ALU.subtract
                                     ).then_inc(S.nlo_ready, 1)

            def finish(k, kb, half, s):
                ve.wait_ge(S.mm2_psum, SUBS * k + s + 1)
                if s == 0:
                    ve.wait_ge(S.resb_ready, SUBS * (k + 1))
                    if not isinstance(half, int) or half >= 1:
                        ve.wait_ge(o_stored[kb], 16 * SUBS * half)
                ve.scalar_tensor_tensor(orow[:, kb, s, :], banks[2 + s % 3][:, 0:D], grow[:, kb, s, D + 3:D + 4],
                                        resb[:, kb, s, :], ALU.add, ALU.add).then_inc(S.final_done, 1)

            def next_round(q, v):
                take_digit(q, v)
                if v < STEPS - 1:
                    count_above(q, v + 1)
                else:
                    mark(q)

            def begin(q):
                begin_search(q)
                count_above(q, 0)

            begin(0)
            for v in range(STEPS):
                next_round(0, v)
            place_tokens(0)
            write_list(0, 0)
            begin(1)
            next_round(1, 0)
            next_round(1, 1)
            ve.wait_ge(w_loaded[0], 64)
            next_round(1, 2)
            low_nbT(0)
            next_round(1, 3)

            def expert(e, half, b, more, more2):
                q, k = e + 1, 2 * e
                if more:
                    next_round(q, 4)
                    next_round(q, 5)
                prepare_sum(k, 0, b)
                if more:
                    next_round(q, 6)
                    next_round(q, 7)
                for s in range(SUBS):
                    if more and s < 3:
                        next_round(q, 8 + s)
                    finish(k, 0, e, s)
                    if s == 0:
                        prepare_sum(k + 1, 1, b)
                    if s == 1:
                        low_nbT(k + 1)
                if more:
                    place_tokens(q)
                    write_list(q, 1 - b)
                    if more2:
                        begin(q + 1)
                    wload(ve, half, b)
                for s in range(SUBS):
                    if more2:
                        next_round(q + 1, s)
                    finish(k + 1, 1, e, s)
                    if more and s == 2:
                        low_nbT(k + 2)

            def wload(eng, half, b):
                eng.wait_ge(w_loaded[1 - b], 64 * (half + 1 + b))

            experts(ve, expert)

        @block.tensor
        def _(pe):
            mm = pe.matmul

            def fold_weights():
                pe.wait_ge(S.prep_dve, OPERANDS)
                for n, (wa, wpT, bias) in enumerate(((wk, wkpT, BK), (wq, wqpT, BQ))):
                    for k in range(KC):
                        for c in range(KC):
                            x = mm(banks[4 + n][:, k * D:(k + 1) * D], wa[:, c, k * P:(k + 1) * P], wpT[:, c, :],
                                   start=(c == 0), stop=(c == KC - 1))
                    for k in range(KC):
                        for c in range(KC):
                            x = mm(banks[6][:, 2 * n + k:2 * n + k + 1], wpT[:, c, k * P:(k + 1) * P],
                                   vecs[:, bias, c:c + 1], start=(c == 0), stop=(c == KC - 1))
                    if n == 1:
                        x.then_inc(S.prep_pe, 2)
                for c in range(KC):
                    x = mm(banks[3][:, 0:D], mean_w[:, :], gwo[:, c, :], start=(c == 0), stop=(c == KC - 1))
                for c in range(KC):
                    x = mm(banks[3][:, D:2 * D], lnb_bc[:, c, :], woT[:, c, :], start=(c == 0), stop=(c == KC - 1))
                x.then_inc(S.prep_pe, 2)

            def embed_T(m, s):
                if s == 0:
                    pe.wait_ge(e_rows[m.b], 16 * SUBS * (m.half + 1))
                wait_after(pe, S.eT_ready, SUBS * m.n + s - 1)
                for k, (a, n) in enumerate(WCH):
                    x = pe.transpose(banks[s % 2][0:n, k * P:(k + 1) * P], erow[:, m.b, s, a:a + n], ident[:, :])
                x.then_inc(S.eT_psum, 1)

            def embed_project(m, s):
                pe.wait_ge(S.eT_ready, SUBS * m.n + s + 1)
                if s % 2 == 0:
                    wait_after(pe, S.r1_summed, 2 * m.n + s // 2)
                for k, (a, n) in enumerate(WCH):
                    x = mm(banks[2][:, (s % 2) * D:(s % 2 + 1) * D], eT[0:n, s % 2, k * P:(k + 1) * P], proj[0:n, k, :],
                           start=(k == 0), stop=(k == len(WCH) - 1))
                x.then_inc(S.h0_psum, 1)

            def turn(dst_bank, src, k):
                for s in range(SUBS):
                    x = pe.transpose(banks[dst_bank][:, s * P:(s + 1) * P], src[:, s, k * P:(k + 1) * P], ident[:, :])
                return x

            def memory_T(m):
                pe.wait_ge(S.xhat_ready, SUBS * (m.n + 1))
                for k in range(KC):
                    wait_after(pe, S.bound_ready, 4 * m.n - 2 + 2 * k)
                    turn(3 + k, xhat[:, m.b], k).then_inc(S.xT_psum, 1)

            def project_kqv(m, w):
                for c in range(KC):
                    n = 2 * w + c
                    bank = (5, 3, 4, 5, 3, 4)[n]
                    if n == 0:
                        pe.wait_ge(S.xT_ready, 2 * m.n + 2)
                    if n == 0:
                        wait_after(pe, S.tanh_done, 4 * m.n)
                    if n >= 3:
                        pe.wait_ge(S.tanh_done, 4 * m.n + n - 2)
                    for k in range(KC):
                        x = mm(banks[bank][:, :], wcomb[:, w, k, c * P:(c + 1) * P], xT[:, k, :],
                               start=(k == 0), stop=(k == KC - 1))
                    x.then_inc(S.kqv_psum, 1)

            def retrieved_T(m, embed):
                pe.wait_ge(S.retrieved, m.n + 1)
                for s in range(SUBS):
                    if s % 2 == 0 and embed:
                        pe.wait_ge(S.eT_ready, SUBS * embed.n + 3 + s // 2)
                    for k in range(KC):
                        x = pe.transpose(banks[s // 2][:, (s % 2) * D + k * P:(s % 2) * D + (k + 1) * P],
                                         ret[:, m.b, k, s * P:(s + 1) * P], ident[:, :])
                    x.then_inc(S.rT_psum, 1)

            def mix_out(m, pair):
                pe.wait_ge(S.r_stats, SUBS * m.n + 2 * pair + 2)
                if pair == 1:
                    wait_after(pe, S.scores_saved, m.n)
                for s in (2 * pair, 2 * pair + 1):
                    for k in range(KC):
                        x = mm(banks[6 + pair][:, (s % 2) * D:(s % 2 + 1) * D], ret[:, m.b, k, s * P:(s + 1) * P],
                               wout[:, k, :], start=(k == 0), stop=(k == KC - 1))
                    x.then_inc(S.wo_psum, 1)

            def mix_T(m):
                pe.wait_ge(S.nhat_ready, SUBS * (m.n + 1))
                for k in range(KC):
                    turn(6 + k, nhat, k).then_inc(S.nT_psum, 1)

            def route_scores(m):
                pe.wait_ge(S.nT_ready, 2 * m.n + 2)
                for k in range(KC):
                    x = mm(banks[6][0:E, :], centT[:, k, :], nT[:, k, :], start=(k == 0), stop=(k == KC - 1))
                x.then_inc(S.scoreT_psum, 1)

            def route_T(m):
                pe.wait_ge(S.scoreT_ready, m.n + 1)
                pe.sem_inc(S.pe_go, 1)
                for s in range(SUBS):
                    x = pe.transpose(banks[7][:, s * E:(s + 1) * E], scoreT[:, s * P:(s + 1) * P], ident[0:E, 0:E])
                x.then_inc(S.scores_psum, 1)

            def step(embed, memory, mix, route, gather):
                if memory:
                    if isinstance(memory.n, int) and memory.n == 0:
                        pe.wait_ge(S.prep_dve, FOLDED)
                    memory_T(memory)
                if embed:
                    embed_T(embed, 0)
                    embed_T(embed, 1)
                if memory:
                    project_kqv(memory, 0)
                if embed:
                    embed_project(embed, 0)
                    embed_project(embed, 1)
                if embed and not memory:
                    fold_weights()
                if memory:
                    project_kqv(memory, 1)
                if route:
                    mix_T(route)
                if embed:
                    embed_T(embed, 2)
                    embed_T(embed, 3)
                if memory:
                    project_kqv(memory, 2)
                if mix:
                    retrieved_T(mix, embed)
                if route:
                    route_scores(route)
                if embed:
                    embed_project(embed, 2)
                    embed_project(embed, 3)
                if route:
                    route_T(route)
                if mix:
                    mix_out(mix, 0)
                    mix_out(mix, 1)

            pe.wait_ge(S.consts, constants[0])
            pe.wait_ge(S.prep_dve, SCALED)
            pipeline(pe, step)

            def count_round(q, v):
                n = 3 if v == 0 else 7
                pe.wait_ge(S.cnt_ready, STEPS * q + v + 1)
                mm(banks[7][:, 0:n], ones16[:, :], cnt[:, 0:n], start=True, stop=True).then_inc(S.cnt_psum, 1)

            def rank_round(q):
                pe.wait_ge(S.gteq_ready, 2 * q + 2)
                g = gteq[:, :, :].rearrange("p g n -> p (g n)")
                mm(banks[7][:, 128:128 + 2 * NT], later16[:, :], g, start=True, stop=True)
                mm(banks[7][:, 128 + 2 * NT:128 + 4 * NT], ones16[:, :], g, start=True, stop=True
                   ).then_inc(S.rank_psum, 1)

            def list_round(q):
                pe.wait_ge(S.onehot_ready, q + 1)
                for j in range(NT):
                    x = mm(banks[7][:, 64:64 + 2 * CT_], onehot[:, :, j], tokhot[:, j, :],
                           start=(j == 0), stop=(j == NT - 1))
                x.then_inc(S.list_psum, 1)

            def ffn_T(k, kb):
                pe.wait_ge(S.nb_ready, SUBS * (k + 1))
                wait_after(pe, S.nbT_ready, 2 * k)
                for c in range(KC):
                    turn(5 + c, nb, c).then_inc(S.nbT_psum, 1)

            def up(k, b, f):
                n = FC * k + f
                if f == 0:
                    pe.wait_ge(S.nhi_ready, 2 * k + 2)
                wait_after(pe, S.gelu_done, n - 1)
                for w, rows in ((w1hi, nhi), (w1lo, nhi), (w1hi, nlo)):
                    if f == 0 and rows is nlo:
                        pe.wait_ge(S.nlo_ready, 2 * k + 2)
                    for c in range(KC):
                        x = mm(banks[f % 2][:, :], w[:, b, c, f * P:(f + 1) * P], rows[:, c, :],
                               start=(w is w1hi and rows is nhi and c == 0), stop=(rows is nlo and c == KC - 1))
                x.then_inc(S.mm1_psum, 1)

            def down(k, kb, b, s):
                if s == 0:
                    wait_after(pe, S.final_done, SUBS * k)
                if s == 3:
                    pe.wait_ge(S.final_done, SUBS * k + 1)
                for f in range(FC):
                    if s == 0 and f >= FC - 2:
                        pe.wait_ge(S.gelu_done, FC * k + f + 1)
                    x = mm(banks[2 + s % 3][:, 0:D], hT[:, f, s * P:(s + 1) * P],
                           w2s[:, b, f, :], start=(f == 0), stop=(f == FC - 1))
                x.then_inc(S.mm2_psum, 1)

            for v in range(STEPS):
                count_round(0, v)
            rank_round(0)
            list_round(0)
            count_round(1, 0)
            count_round(1, 1)
            count_round(1, 2)
            ffn_T(0, 0)
            count_round(1, 3)

            def expert(e, half, b, more, more2):
                q, k = e + 1, 2 * e
                pe.wait_ge(S.w1lo_ready, 2 * e + 2)
                pe.wait_ge(w_loaded[b], 64 * (half + 1))
                for f in range(FC):
                    up(k, b, f)
                    if more and f % 2:
                        count_round(q, 4 + f // 2)
                for s in range(SUBS):
                    down(k, 0, b, s)
                    if s == 1:
                        ffn_T(k + 1, 1)
                    if more and s < 3:
                        count_round(q, 8 + s)
                if more:
                    rank_round(q)
                for f in range(FC):
                    up(k + 1, b, f)
                    if more and f == 7:
                        list_round(q)
                for s in range(SUBS):
                    down(k + 1, 1, b, s)
                    if more and s == 2:
                        ffn_T(k + 2, 0)
                    if more2:
                        count_round(q + 1, s)

            experts(pe, expert)


def _link(eng, sm, before, count, ins):
    count[0] += 1
    ins.then_inc(sm, 1)
    eng.wait_ge(sm, before + count[0])


def kernel(**inputs):
    import numpy as np
    import concourse.bacc as bacc
    from concourse.bass_utils import run_bass_kernel_spmd as run

    g = {k: np.asarray(v) for k, v in inputs.items()}

    def flat(a):
        return np.ascontiguousarray(a)

    x = g["x"]
    T = x.size
    embs = [g[f"L0_tok_emb{i}"] for i in range(4)]
    width = sum(e.shape[1] for e in embs)
    table = np.zeros((sum(e.shape[0] for e in embs) + 1, width), np.float32)
    r = c = 0
    for e in embs:
        table[r:r + e.shape[0], c:c + e.shape[1]] = e
        r, c = r + e.shape[0], c + e.shape[1]

    def vec(a):
        return flat(a.reshape(-1, P).T)

    a = {
        "tok": flat(x.reshape(T // P, P).T),
        "table": table,
        "projT": flat(np.concatenate([g[f"L0_tok_proj{i}"].T for i in range(4)], axis=0)),
        "wk": flat(g["L0_attn_Wk"]), "wq": flat(g["L0_attn_Wq"]),
        "wkpT": flat(g["L0_attn_Wkp"].T), "wqpT": flat(g["L0_attn_Wqp"].T),
        "wvT": flat(g["L0_attn_Wv"].T), "woT": flat(g["L0_attn_Wo"].T),
        "bo": flat(g["L0_attn_bo"]),
        "vecs": flat(np.stack([vec(g["L0_" + n]) for n in (
            "attn_bk", "attn_bv", "attn_bq", "attn_bkp", "attn_bqp", "attn_phase_scale",
            "attn_ln_g", "attn_ln_b", "ffn_ln_g", "ffn_ln_b")], axis=1)),
        "centT": flat(g["L0_ffn_centroids"].T),
        "w1": flat(g["L0_ffn_w1"]), "w2": flat(g["L0_ffn_w2"]),
        "b1": flat(g["L0_ffn_b1"].reshape(g["L0_ffn_b1"].shape[0], -1, P).transpose(0, 2, 1)),
        "b2": flat(g["L0_ffn_b2"]),
    }
    nc = bacc.Bacc("TRN2", target_bir_lowering=False, num_devices=1)
    t = {n: nc.dram_tensor(f"in_{n}", v.shape, mybir.dt.from_np(v.dtype), kind="ExternalInput").ap()
         for n, v in a.items()}
    t["out"] = nc.dram_tensor("out_rows", (T, D), F32, kind="ExternalOutput").ap()
    tower(nc, t)
    res = run(nc, [{f"in_{n}": v for n, v in a.items()}], core_ids=[0])
    return res.results[0]["out_rows"].reshape(*x.shape, D)
```
